# Optimizing a Trainium2 kernel written in Bass

```python
import numpy as np
import jax
import jax.numpy as jnp

def _softmax(x, axis=-1):
    return jax.nn.softmax(x, axis=axis)

def _gelu(x):
    return jax.nn.gelu(x, approximate=True)

def _silu(x):
    return jax.nn.silu(x)

def _sigmoid(x):
    return jax.nn.sigmoid(x)

def _layernorm(x, axis=-1, eps=1e-05):
    m = jnp.mean(x, axis=axis, keepdims=True)
    v = jnp.var(x, axis=axis, keepdims=True)
    return (x - m) / jnp.sqrt(v + eps)

def _scatter_add(tgt, idx, src, axis=0):
    return tgt.at[idx].add(src)

def _segment_sum(src, seg, n):
    return jax.ops.segment_sum(src, seg, n)
kernel_name = 'mk_dlrm_tower_d1_rec_r8_cffe1a'

def setup_inputs(seed: int=0):
    np.random.seed(seed)
    _w = jnp.asarray

    def _rec_inputs():
        import jax
        import jax.numpy as jnp
        _tk = jax.random.key(seed)
        ids = jnp.stack([jax.random.randint(jax.random.fold_in(_tk, 200 + f), (2048,), 0, v, jnp.int32) for f, v in enumerate([125000, 125000, 12500, 125000, 1250, 1000, 12500, 1250, 1000, 1000, 1000, 1000, 1250, 1250, 1000, 1250, 12500, 12500, 12500, 1000, 12500, 1000, 1000, 12500, 1000, 12500])], axis=1)
        tbl_0 = 0.05 * jax.random.normal(jax.random.fold_in(_tk, 500 + 0), (125000, 64), jnp.float32)
        tbl_1 = 0.05 * jax.random.normal(jax.random.fold_in(_tk, 500 + 1), (125000, 64), jnp.float32)
        tbl_2 = 0.05 * jax.random.normal(jax.random.fold_in(_tk, 500 + 2), (12500, 64), jnp.float32)
        tbl_3 = 0.05 * jax.random.normal(jax.random.fold_in(_tk, 500 + 3), (125000, 64), jnp.float32)
        tbl_4 = 0.05 * jax.random.normal(jax.random.fold_in(_tk, 500 + 4), (1250, 64), jnp.float32)
        tbl_5 = 0.05 * jax.random.normal(jax.random.fold_in(_tk, 500 + 5), (1000, 64), jnp.float32)
        tbl_6 = 0.05 * jax.random.normal(jax.random.fold_in(_tk, 500 + 6), (12500, 64), jnp.float32)
        tbl_7 = 0.05 * jax.random.normal(jax.random.fold_in(_tk, 500 + 7), (1250, 64), jnp.float32)
        tbl_8 = 0.05 * jax.random.normal(jax.random.fold_in(_tk, 500 + 8), (1000, 64), jnp.float32)
        tbl_9 = 0.05 * jax.random.normal(jax.random.fold_in(_tk, 500 + 9), (1000, 64), jnp.float32)
        tbl_10 = 0.05 * jax.random.normal(jax.random.fold_in(_tk, 500 + 10), (1000, 64), jnp.float32)
        tbl_11 = 0.05 * jax.random.normal(jax.random.fold_in(_tk, 500 + 11), (1000, 64), jnp.float32)
        tbl_12 = 0.05 * jax.random.normal(jax.random.fold_in(_tk, 500 + 12), (1250, 64), jnp.float32)
        tbl_13 = 0.05 * jax.random.normal(jax.random.fold_in(_tk, 500 + 13), (1250, 64), jnp.float32)
        tbl_14 = 0.05 * jax.random.normal(jax.random.fold_in(_tk, 500 + 14), (1000, 64), jnp.float32)
        tbl_15 = 0.05 * jax.random.normal(jax.random.fold_in(_tk, 500 + 15), (1250, 64), jnp.float32)
        tbl_16 = 0.05 * jax.random.normal(jax.random.fold_in(_tk, 500 + 16), (12500, 64), jnp.float32)
        tbl_17 = 0.05 * jax.random.normal(jax.random.fold_in(_tk, 500 + 17), (12500, 64), jnp.float32)
        tbl_18 = 0.05 * jax.random.normal(jax.random.fold_in(_tk, 500 + 18), (12500, 64), jnp.float32)
        tbl_19 = 0.05 * jax.random.normal(jax.random.fold_in(_tk, 500 + 19), (1000, 64), jnp.float32)
        tbl_20 = 0.05 * jax.random.normal(jax.random.fold_in(_tk, 500 + 20), (12500, 64), jnp.float32)
        tbl_21 = 0.05 * jax.random.normal(jax.random.fold_in(_tk, 500 + 21), (1000, 64), jnp.float32)
        tbl_22 = 0.05 * jax.random.normal(jax.random.fold_in(_tk, 500 + 22), (1000, 64), jnp.float32)
        tbl_23 = 0.05 * jax.random.normal(jax.random.fold_in(_tk, 500 + 23), (12500, 64), jnp.float32)
        tbl_24 = 0.05 * jax.random.normal(jax.random.fold_in(_tk, 500 + 24), (1000, 64), jnp.float32)
        tbl_25 = 0.05 * jax.random.normal(jax.random.fold_in(_tk, 500 + 25), (12500, 64), jnp.float32)
        _rk = jax.random.fold_in(_tk, 7)
        r_dense_t = 7.22013e-05 + 1.00017 * jax.random.normal(jax.random.fold_in(_rk, 101), (2048, 256), jnp.float32)
        W_top1 = 0.0360844 * jax.random.normal(jax.random.fold_in(_tk, 801), (768, 512), jnp.float32)
        W_top2 = 0.0441942 * jax.random.normal(jax.random.fold_in(_tk, 802), (512, 256), jnp.float32)
        W_top3 = 0.0625 * jax.random.normal(jax.random.fold_in(_tk, 803), (256, 1), jnp.float32)
        b_top1 = jnp.zeros((512,), jnp.float32)
        b_top2 = jnp.zeros((256,), jnp.float32)
        return (r_dense_t, ids, tbl_0, tbl_1, tbl_2, tbl_3, tbl_4, tbl_5, tbl_6, tbl_7, tbl_8, tbl_9, tbl_10, tbl_11, tbl_12, tbl_13, tbl_14, tbl_15, tbl_16, tbl_17, tbl_18, tbl_19, tbl_20, tbl_21, tbl_22, tbl_23, tbl_24, tbl_25, W_top1, b_top1, W_top2, b_top2, W_top3)
    r_dense_t, ids, tbl_0, tbl_1, tbl_2, tbl_3, tbl_4, tbl_5, tbl_6, tbl_7, tbl_8, tbl_9, tbl_10, tbl_11, tbl_12, tbl_13, tbl_14, tbl_15, tbl_16, tbl_17, tbl_18, tbl_19, tbl_20, tbl_21, tbl_22, tbl_23, tbl_24, tbl_25, W_top1, b_top1, W_top2, b_top2, W_top3 = _rec_inputs()

    def _L0_rec_setup():
        import jax, jax.numpy as jnp
        import numpy as np
        EPS = 1e-05
        NI = 33
        TRIL_I, TRIL_J = np.tril_indices(NI, k=-1)

        def layer_norm(x, g, b):
            m = jnp.mean(x, axis=-1, keepdims=True)
            v = jnp.mean(jnp.square(x - m), axis=-1, keepdims=True)
            return (x - m) * jax.lax.rsqrt(v + EPS) * g + b
        key = jax.random.key(seed)
        ks = jax.random.split(key, 8)
        B, D_DENSE, N_SP, D_SP = (4096, 256, 26, 64)
        E, PROJ, MAXD, NFLAT = (128, 32, 512, 528)
        dense_t = jax.random.normal(ks[0], (B, D_DENSE), dtype=jnp.float32)
        sparse_t = jax.random.normal(ks[1], (B, N_SP, D_SP), dtype=jnp.float32)
        Wd = jax.random.normal(ks[2], (E, D_DENSE), dtype=jnp.float32) / np.sqrt(D_DENSE)
        Ws = jax.random.normal(ks[3], (E, D_SP), dtype=jnp.float32) / np.sqrt(D_SP)
        Wsi = jax.random.normal(ks[4], (PROJ, N_SP), dtype=jnp.float32) / np.sqrt(N_SP)
        Wl = jax.random.normal(ks[5], (MAXD, NFLAT), dtype=jnp.float32) / np.sqrt(NFLAT)
        gd = jnp.ones((E,), jnp.float32)
        bd = jnp.zeros((E,), jnp.float32)
        gs = jnp.ones((E,), jnp.float32)
        bs = jnp.zeros((E,), jnp.float32)
        gsi = jnp.ones((PROJ,), jnp.float32)
        bsi = jnp.zeros((PROJ,), jnp.float32)
        gl = jnp.ones((MAXD,), jnp.float32)
        bl = jnp.zeros((MAXD,), jnp.float32)
        return {'dense_t': dense_t, 'sparse_t': sparse_t, 'Wd': Wd, 'gd': gd, 'bd': bd, 'Ws': Ws, 'gs': gs, 'bs': bs, 'Wsi': Wsi, 'gsi': gsi, 'bsi': bsi, 'Wl': Wl, 'gl': gl, 'bl': bl, 'dims_in_use': 384}
    _L0_rec_all = _L0_rec_setup()
    _L0_rec_in = {k: v for k, v in _L0_rec_all.items() if k in ('Wd', 'gd', 'bd', 'Ws', 'gs', 'bs', 'Wsi', 'gsi', 'bsi', 'Wl', 'gl', 'bl')}
    del _L0_rec_all
    return {'r_dense_t': r_dense_t, 'ids': ids, 'tbl_0': tbl_0, 'tbl_1': tbl_1, 'tbl_2': tbl_2, 'tbl_3': tbl_3, 'tbl_4': tbl_4, 'tbl_5': tbl_5, 'tbl_6': tbl_6, 'tbl_7': tbl_7, 'tbl_8': tbl_8, 'tbl_9': tbl_9, 'tbl_10': tbl_10, 'tbl_11': tbl_11, 'tbl_12': tbl_12, 'tbl_13': tbl_13, 'tbl_14': tbl_14, 'tbl_15': tbl_15, 'tbl_16': tbl_16, 'tbl_17': tbl_17, 'tbl_18': tbl_18, 'tbl_19': tbl_19, 'tbl_20': tbl_20, 'tbl_21': tbl_21, 'tbl_22': tbl_22, 'tbl_23': tbl_23, 'tbl_24': tbl_24, 'tbl_25': tbl_25, 'W_top1': W_top1, 'b_top1': b_top1, 'W_top2': W_top2, 'b_top2': b_top2, 'W_top3': W_top3, 'L0_rec_Wd': _L0_rec_in['Wd'], 'L0_rec_gd': _L0_rec_in['gd'], 'L0_rec_bd': _L0_rec_in['bd'], 'L0_rec_Ws': _L0_rec_in['Ws'], 'L0_rec_gs': _L0_rec_in['gs'], 'L0_rec_bs': _L0_rec_in['bs'], 'L0_rec_Wsi': _L0_rec_in['Wsi'], 'L0_rec_gsi': _L0_rec_in['gsi'], 'L0_rec_bsi': _L0_rec_in['bsi'], 'L0_rec_Wl': _L0_rec_in['Wl'], 'L0_rec_gl': _L0_rec_in['gl'], 'L0_rec_bl': _L0_rec_in['bl']}

def reference(r_dense_t, ids, tbl_0, tbl_1, tbl_2, tbl_3, tbl_4, tbl_5, tbl_6, tbl_7, tbl_8, tbl_9, tbl_10, tbl_11, tbl_12, tbl_13, tbl_14, tbl_15, tbl_16, tbl_17, tbl_18, tbl_19, tbl_20, tbl_21, tbl_22, tbl_23, tbl_24, tbl_25, W_top1, b_top1, W_top2, b_top2, W_top3, L0_rec_Wd, L0_rec_gd, L0_rec_bd, L0_rec_Ws, L0_rec_gs, L0_rec_bs, L0_rec_Wsi, L0_rec_gsi, L0_rec_bsi, L0_rec_Wl, L0_rec_gl, L0_rec_bl):
    import jax
    import jax.numpy as jnp

    def _L0_rec_ref(dense_t, sparse_t, Wd, gd, bd, Ws, gs, bs, Wsi, gsi, bsi, Wl, gl, bl, dims_in_use):
        import jax, jax.numpy as jnp
        import numpy as np
        EPS = 1e-05
        NI = 33
        TRIL_I, TRIL_J = np.tril_indices(NI, k=-1)

        def layer_norm(x, g, b):
            m = jnp.mean(x, axis=-1, keepdims=True)
            v = jnp.mean(jnp.square(x - m), axis=-1, keepdims=True)
            return (x - m) * jax.lax.rsqrt(v + EPS) * g + b
        x = layer_norm(dense_t @ Wd.T, gd, bd)
        y = layer_norm(jnp.einsum('bnd,ed->bne', sparse_t, Ws), gs, bs)
        y = jnp.einsum('bne,pn->bep', y, Wsi)
        y = layer_norm(y, gsi, bsi)
        y = jnp.swapaxes(y, 1, 2)
        T = jnp.concatenate([x[:, None, :], y], axis=1)
        Z = jnp.einsum('bnd,bmd->bnm', T, T)
        Zflat = Z[:, TRIL_I, TRIL_J]
        out = layer_norm(Zflat @ Wl.T, gl, bl)
        maxd = out.shape[-1]
        mask = (jnp.arange(maxd) < dims_in_use).astype(out.dtype)
        return out * mask
    e = jnp.stack([tbl_0[ids[:, 0]], tbl_1[ids[:, 1]], tbl_2[ids[:, 2]], tbl_3[ids[:, 3]], tbl_4[ids[:, 4]], tbl_5[ids[:, 5]], tbl_6[ids[:, 6]], tbl_7[ids[:, 7]], tbl_8[ids[:, 8]], tbl_9[ids[:, 9]], tbl_10[ids[:, 10]], tbl_11[ids[:, 11]], tbl_12[ids[:, 12]], tbl_13[ids[:, 13]], tbl_14[ids[:, 14]], tbl_15[ids[:, 15]], tbl_16[ids[:, 16]], tbl_17[ids[:, 17]], tbl_18[ids[:, 18]], tbl_19[ids[:, 19]], tbl_20[ids[:, 20]], tbl_21[ids[:, 21]], tbl_22[ids[:, 22]], tbl_23[ids[:, 23]], tbl_24[ids[:, 24]], tbl_25[ids[:, 25]]], axis=1)
    z = _L0_rec_ref(r_dense_t, e, L0_rec_Wd, L0_rec_gd, L0_rec_bd, L0_rec_Ws, L0_rec_gs, L0_rec_bs, L0_rec_Wsi, L0_rec_gsi, L0_rec_bsi, L0_rec_Wl, L0_rec_gl, L0_rec_bl, 384)
    z = z.reshape(z.shape[0], -1)
    h = jnp.concatenate([z, r_dense_t], axis=1)
    h = jnp.maximum(h @ W_top1 + b_top1, 0.0)
    h = jnp.maximum(h @ W_top2 + b_top2, 0.0)
    y = h @ W_top3
    return y

_drawn_inputs = setup_inputs


def setup_inputs(seed=0):
    import zlib

    import numpy as np

    out = dict(_drawn_inputs(seed))
    spreads = {'b_top1': (0.0, 0.1),
     'b_top2': (0.0, 0.1),
     'L0_rec_gd': (1.0, 0.6),
     'L0_rec_bd': (0.0, 0.8),
     'L0_rec_gs': (1.0, 0.6),
     'L0_rec_bs': (0.0, 0.1),
     'L0_rec_gsi': (1.0, 0.2),
     'L0_rec_bsi': (0.0, 0.1),
     'L0_rec_gl': (1.0, 0.2),
     'L0_rec_bl': (0.0, 0.1)}
    factors = {}
    for name, (base, spread) in spreads.items():
        noise = np.random.default_rng([zlib.crc32(name.encode()), seed]).standard_normal(out[name].shape)
        drawn = base * np.exp(spread * noise) if base else spread * noise
        out[name] = jnp.asarray(drawn.astype(out[name].dtype))
    for name, factor in factors.items():
        out[name] = (out[name] * factor).astype(out[name].dtype)
    return out
```

```python
import concourse.bass as bass
import numpy as np
from concourse import mybir
from contextlib import ExitStack

BATCH = 2048
NF = 26
DSP = 64
E = 128
PROJ = 32
DD = 256
MAXD = 512
USED = 384
H1, H2 = 512, 256
EPS = 1e-5

P = 128
TILE = 128
TILES = BATCH // TILE
GROUP = 4
CHUNK = 4 * GROUP
CHUNKS = TILE // CHUNK
ROWS = GROUP * NF
COLS = PROJ + 2
QB = PROJ // 4
ZK = QB + 1
UK = USED // P
DK = DD // P
PIECES = [(0, 4), (4, 7), (7, 10), (10, 13)]
SLOTS = TILE // 4
MOVES = 4 * 4 + 2 * 4 + 1

_FIELDS = [("ident", P), ("ident_sum", P), ("delta_p", PROJ), ("delta_q", QB * PROJ), ("bsi_p", 1),
           ("bsi_q", QB), ("gsi_p", 1), ("gsi_q", QB), ("gsi_free", PROJ), ("ws", E), ("wsi", P),
           ("gs", E), ("gd", 1), ("bd", 1), ("gl", UK), ("bl", UK), ("b1", H1 // P), ("b2", H2 // P),
           ("w3", H2 // P), ("wd", DK * E)]
FIELD = {}
NPAR = 0
for _name, _width in _FIELDS:
    FIELD[_name] = (NPAR, NPAR + _width)
    NPAR += _width


def build(nc, tables, ids, params, bs_row, dense_t, wl, w1, w2, out):
    fp32 = mybir.dt.float32
    i32 = mybir.dt.int32
    ALU = mybir.AluOpType
    ACT = mybir.ActivationFunctionType
    AX = mybir.AxisListType

    with ExitStack() as ctx:
        def sb(name, shape, dt=fp32):
            return ctx.enter_context(nc.sbuf_tensor(name, shape, dt))

        def bank(name):
            return ctx.enter_context(nc.psum_tensor(name, [P, 512], fp32))

        def sem(name):
            return ctx.enter_context(nc.semaphore(name))

        par = sb("par", [P, NPAR])
        wl_sb = sb("wl_sb", [P, ZK, MAXD])
        w9 = sb("w9", [P, MAXD])
        w1_sb = sb("w1_sb", [P, UK + DK, H1])
        w2_sb = sb("w2_sb", [P, H1 // P, H2])
        dense_sb = sb("dense_sb", [P, DK, BATCH])
        fold = sb("fold", [P, ZK, P])
        ws_c = sb("ws_c", [P, E])
        wsi_c = sb("wsi_c", [P, P])
        gg = sb("gg", [P, QB])
        means = sb("means", [P, 8])
        ones = sb("ones", [P, PROJ])
        eps_sb = sb("eps_sb", [P, 1])
        x_stats = sb("x_stats", [P, TILES, 6])
        x_mv = sb("x_mv", [P, TILES, 2])
        x_sd = sb("x_sd", [P, TILES])
        x_rs = sb("x_rs", [P, TILES])
        x_t = sb("x_t", [P, BATCH])
        x_sum = sb("x_sum", [P, BATCH])

        idx = [sb(f"idx{i}", [P, NF], i32) for i in range(2)]
        emb = [sb(f"emb{i}", [P, NF, DSP]) for i in range(2)]
        emb_t = [sb(f"emb_t{i}", [P, TILE, NF]) for i in range(2)]
        feat = [sb(f"feat{i}", [P, TILE, COLS]) for i in range(2)]
        sq_y = [sb(f"sq_y{i}", [P, 512]) for i in range(2)]
        ss_y = [sb(f"ss_y{i}", [P, 4]) for i in range(2)]
        sd_y = [sb(f"sd_y{i}", [P, 4]) for i in range(2)]
        rs_y = [sb(f"rs_y{i}", [P, 4]) for i in range(2)]
        y_sb = [sb(f"y_sb{i}", [P, 4, E]) for i in range(2)]
        sq_u = [sb(f"sq_u{i}", [P, 512]) for i in range(2)]
        ss_u = [sb(f"ss_u{i}", [P, CHUNK]) for i in range(2)]
        sd_u = [sb(f"sd_u{i}", [P, CHUNK]) for i in range(2)]
        rs_u = [sb(f"rs_u{i}", [P, CHUNK]) for i in range(2)]
        z_stage = [sb(f"z_stage{i}", [P, 4, SLOTS, QB]) for i in range(2)]
        z_extra = [sb(f"z_extra{i}", [P, 2, SLOTS]) for i in range(2)]
        z_k = [sb(f"z_k{i}", [P, 4, SLOTS, QB]) for i in range(2)]
        z_9 = [sb(f"z_9{i}", [P, 4, SLOTS]) for i in range(2)]
        zn = sb("zn", [P, USED])
        l_stats = sb("l_stats", [P, 6])
        l_mv = sb("l_mv", [P, 2])
        l_sd = sb("l_sd", [P, 1])
        l_rs = sb("l_rs", [P, 1])
        zn_t = sb("zn_t", [P, UK, TILE])
        h1_t = sb("h1_t", [P, H1 // P, TILE])
        h2_t = sb("h2_t", [P, H2 // P, TILE])
        out_sb = sb("out_sb", [1, BATCH])
        xn = feat[0][:, :, :].rearrange("p a b -> p (a b)")[:, 0:BATCH].rearrange("p (t e) -> p t e", t=TILES)

        p_y = [bank(f"p_y{i}") for i in range(2)]
        p_u = [bank(f"p_u{i}") for i in range(2)]
        p_z = [bank(f"p_z{i}") for i in range(2)]
        p_t = bank("p_t")
        p_o = bank("p_o")

        def F(name, lo=0, hi=P):
            a, b = FIELD[name]
            return par[lo:hi, a:b]

        s_par = sem("s_par")
        s_dense = sem("s_dense")
        s_wl = sem("s_wl")
        s_w12 = sem("s_w12")
        s_bsrow = sem("s_bsrow")
        s_idx = [sem(f"s_idx{i}") for i in range(2)]
        s_gather = [sem(f"s_gather{i}") for i in range(2)]
        s_start = sem("s_start")
        s_clear = sem("s_clear")
        s_xmm = sem("s_xmm")
        s_xstat = sem("s_xstat")
        s_xmv = sem("s_xmv")
        s_xsd = sem("s_xsd")
        s_xrs = sem("s_xrs")
        s_xn = sem("s_xn")
        s_xtr = sem("s_xtr")
        s_xt = sem("s_xt")
        s_xsmm = sem("s_xsmm")
        s_xs = sem("s_xs")
        s_mean = sem("s_mean")
        s_cen = sem("s_cen")
        s_wsimm = sem("s_wsimm")
        s_wsi = sem("s_wsi")
        s_fold = sem("s_fold")
        s_w9mm = sem("s_w9mm")
        s_w9 = sem("s_w9")
        s_gg = sem("s_gg")
        s_wls = sem("s_wls")
        s_y = sem("s_y")
        s_sqy = sem("s_sqy")
        s_ssy = sem("s_ssy")
        s_sdy = sem("s_sdy")
        s_rsy = sem("s_rsy")
        s_ysb = sem("s_ysb")
        s_u = sem("s_u")
        s_squ = sem("s_squ")
        s_ssu = sem("s_ssu")
        s_sdu = sem("s_sdu")
        s_rsu = sem("s_rsu")
        s_feat = sem("s_feat")
        s_z = sem("s_z")
        s_zs = sem("s_zs")
        s_tr = sem("s_tr")
        s_embt = sem("s_embt")
        s_zk = [sem(f"s_zk{i}") for i in range(2)]
        s_l = sem("s_l")
        s_lst = sem("s_lst")
        s_lmv = sem("s_lmv")
        s_lsd = sem("s_lsd")
        s_lrs = sem("s_lrs")
        s_zn = sem("s_zn")
        s_zt = sem("s_zt")
        s_znt = sem("s_znt")
        s_h1 = sem("s_h1")
        s_h1t = sem("s_h1t")
        s_h2 = sem("s_h2")
        s_h2t = sem("s_h2t")
        s_o = sem("s_o")
        s_osb = sem("s_osb")
        s_out = sem("s_out")

        block = ctx.enter_context(nc.Block())

        def need(eng, s, value):
            if not isinstance(value, int) or value > 0:
                eng.wait_ge(s, value)

        def over_tiles(eng, tile):
            for t in (0, 1):
                tile(t, t, 0)
            with eng.Fori(1, TILES // 2 - 1) as i:
                for par_ in range(2):
                    tile(i * 2 + par_, None, i, par_)
            for t in range(TILES - 2, TILES + 2):
                tile(t, t, t // 2)

        @block.sync
        def _(sp):
            sp.dma_start(idx[0][:, :], ids[0:TILE, :]).then_inc(s_idx[0], 16)
            sp.dma_start(par[:, :], params).then_inc(s_par, 16)
            sp.dma_start(idx[1][:, :], ids[TILE:2 * TILE, :]).then_inc(s_idx[1], 16)
            sp.dma_start(dense_sb[:, :, :], dense_t.rearrange("(k p) b -> p k b", p=P)).then_inc(s_dense, 16)
            sp.dma_start(wl_sb[:, :, :], wl).then_inc(s_wl, 16)
            for b in range(2):
                sp.dma_start(y_sb[b][ROWS:ROWS + 1, :, :], bs_row).then_inc(s_bsrow, 16)
            sp.dma_start(w1_sb[:, 0:UK, :],
                         w1[0:USED, :].rearrange("(k p) n -> p k n", p=P)).then_inc(s_w12, 16)
            sp.dma_start(w1_sb[:, UK:UK + DK, :],
                         w1[MAXD:MAXD + DD, :].rearrange("(k p) n -> p k n", p=P)).then_inc(s_w12, 16)
            sp.dma_start(w2_sb[:, :, :], w2.rearrange("(k p) n -> p k n", p=P)).then_inc(s_w12, 16)
            sp.wait_ge(s_xs, 4)

            def held(value):
                return value if isinstance(value, int) else sp.snap(value)

            def tile(t, known, uses, b=None):
                b = known % 2 if b is None else b
                if known is None or known + 2 < TILES:
                    row, gathered = held((t + 2) * TILE), held((uses + 1) * (16 * NF))
                    sp.wait_ge(s_gather[b], gathered)
                    sp.dma_start(idx[b][:, :], ids[bass.ds(row, TILE), :]).then_inc(s_idx[b], 16)
                if known is None or 1 <= known <= TILES:
                    o = 1 - b
                    staged, row = held(t * CHUNKS), held((t - 1) * TILE)
                    need(sp, s_zs, staged)
                    for g in range(4):
                        for j in range(4):
                            sp.dma_start(z_k[o][32 * j:32 * j + 32, g, :, :],
                                         z_stage[o][32 * g:32 * g + 32, j, :, :]).then_inc(s_zk[o], 16)
                        for e in range(2):
                            sp.dma_start(z_9[o][32 * e:32 * e + 32, g, :],
                                         z_extra[o][32 * g:32 * g + 32, e, :]).then_inc(s_zk[o], 16)
                    sums = x_sum[64:96, bass.ds(row, TILE)]
                    sp.dma_start(z_9[o][64:96, :, :].rearrange("p g i -> p (g i)"), sums).then_inc(s_zk[o], 16)

            over_tiles(sp, tile)
            sp.wait_ge(s_osb, TILES)
            sp.dma_start(out.rearrange("b a -> a b"), out_sb[:, :]).then_inc(s_out, 16)
            sp.wait_ge(s_out, 16)

        @block.gpsimd
        def _(pool):
            def tile(t, known, uses, b=None):
                if known is not None and known >= TILES:
                    return
                b = known % 2 if b is None else b
                pool.wait_ge(s_idx[b], (uses + 1) * 16)
                need(pool, s_tr, (t - 1) * len(PIECES))
                pool.sem_inc(s_start, 1)
                for n in range(NF):
                    pool.indirect_dma_start(
                        emb[b][:, n, :], None, tables[n],
                        bass.IndirectOffsetOnAxis(ap=idx[b][:, n:n + 1], axis=0)).then_inc(s_gather[b], 16)

            over_tiles(pool, tile)

        @block.tensor
        def _(pe):
            banks = [p_y[0], p_y[1], p_u[0], p_u[1]]
            pe.wait_ge(s_par, 16)
            pe.wait_ge(s_dense, 16)
            wd = F("wd").rearrange("p (k e) -> p k e", k=DK)
            for q in range(4):
                for i in range(4):
                    t = 4 * q + i
                    for k in range(DK):
                        last = pe.matmul(banks[q][:, i * E:i * E + E], dense_sb[:, k, t * TILE:t * TILE + TILE],
                                         wd[:, k, :], start=(k == 0), stop=(k == DK - 1))
                last.then_inc(s_xmm, 1)
            pe.wait_ge(s_cen, 2)
            pe.matmul(p_o[:, 0:P], F("ident_sum", 0, ROWS), wsi_c[0:ROWS, :], start=True, stop=True).then_inc(s_wsimm, 1)
            pe.wait_ge(s_wl, 16)
            pe.wait_ge(s_fold, 6)
            for k in range(ZK):
                last = pe.matmul(p_t[:, :], fold[:, k, :], wl_sb[:, k, :], start=(k == 0), stop=(k == ZK - 1))
            last.then_inc(s_w9mm, 1)
            xbanks = [p_z[0], p_z[1], p_y[0], p_y[1]]
            for q in range(4):
                pe.wait_ge(s_xn, 4 * q + 4 if q < 2 else TILES)
                for i in range(4):
                    last = pe.transpose(xbanks[q][:, i * TILE:i * TILE + TILE], xn[:, 4 * q + i, :], F("ident"))
                last.then_inc(s_xtr, 1)
            pe.wait_ge(s_clear, 1)
            pe.wait_ge(s_wsi, 1)
            for q in range(4):
                pe.wait_ge(s_xt, q + 1)
                if q >= 2:
                    pe.wait_ge(s_xs, q - 1)
                dst = p_u[q % 2]
                pe.matmul(dst[64:96, :], ones[:, :], x_t[:, 512 * q:512 * q + 512],
                          start=True, stop=True).then_inc(s_xsmm, 1)

            def transposes(t, b, k, uses):
                if k == 0:
                    pe.wait_ge(s_gather[b], (uses + 1) * (16 * NF))
                need(pe, s_embt, (t * len(PIECES) + k) * 2)
                a, z = PIECES[k]
                for n in range(a, z):
                    last = pe.transpose(p_t[:, (n - a) * TILE:(n - a + 1) * TILE],
                                        emb[b][:, 2 * n:2 * n + 2, :].rearrange("p n d -> p (n d)"), F("ident"))
                last.then_inc(s_tr, 1)

            pe.wait_ge(s_w9, 1)
            for k in range(len(PIECES)):
                transposes(0, 0, k, 0)
            pe.wait_ge(s_bsrow, 32)
            pe.wait_ge(s_xs, 4)
            pe.wait_ge(s_w12, 48)

            def project(s, c, b):
                for g in range(4):
                    e0 = g * SLOTS + c * GROUP
                    last = pe.matmul(p_y[c % 2][0:ROWS, g * E:g * E + E],
                                     emb_t[b][:, e0:e0 + GROUP, :].rearrange("p a b -> p (a b)"),
                                     ws_c[:, :], start=True, stop=True)
                last.then_inc(s_y, 1)

            def combine(c):
                for g in range(4):
                    last = pe.matmul(p_u[c % 2][:, g * P:g * P + P], y_sb[c % 2][0:ROWS + 1, g, :],
                                     wsi_c[0:ROWS + 1, :], start=True, stop=True)
                last.then_inc(s_u, 1)

            def interact(c, b):
                for e in range(CHUNK):
                    i, g = e // 4, e % 4
                    v = feat[b][:, g * SLOTS + c * GROUP + i, :]
                    last = pe.matmul(p_z[c % 2][32 * g:32 * g + 32, i * COLS:(i + 1) * COLS],
                                     v[:, 0:PROJ], v, start=True, stop=True)
                last.then_inc(s_z, 1)

            def layer(b, ks):
                for k in ks:
                    if k < QB:
                        lhs = z_k[b][:, :, :, k].rearrange("p g i -> p (g i)")
                        rhs = wl_sb[:, k, :]
                    else:
                        lhs = z_9[b][:, :, :].rearrange("p g i -> p (g i)")
                        rhs = w9[:, :]
                    last = pe.matmul(p_o[:, :], lhs, rhs, start=(k == 0), stop=(k == ZK - 1))
                if ks[-1] == ZK - 1:
                    last.then_inc(s_l, 1)

            def tile(t, known, uses, b=None):
                live = known is None or known < TILES
                nxt = known is None or known + 1 < TILES
                prev = known is None or 1 <= known <= TILES
                prev2 = known is None or known >= 2
                b = known % 2 if b is None else b
                o = 1 - b
                for c in range(CHUNKS):
                    s = t * CHUNKS + c
                    if live:
                        if c == 0:
                            need(pe, s_embt, (t + 1) * (2 * len(PIECES)))
                        need(pe, s_ysb, s - 1)
                        project(s, c, b)
                    if live and known != 0 or c == 0 and prev or known == 0 and c >= 1:
                        need(pe, s_ysb, s)
                        need(pe, s_feat, s - 2)
                        combine((c - 1) % CHUNKS)
                    if live and known != 0 or c < 2 and prev or known == 0 and c >= 2:
                        need(pe, s_feat, s - 1)
                        need(pe, s_zs, s - 3)
                        interact((c - 2) % CHUNKS, b if c >= 2 else o)
                    if c == 0 and prev2:
                        pe.wait_ge(s_h1t, (t - 1) * (H1 // P))
                        for m in range(H2 // P):
                            for k in range(H1 // P):
                                last = pe.matmul(p_o[:, m * TILE:(m + 1) * TILE], w2_sb[:, k, m * P:(m + 1) * P],
                                                 h1_t[:, k, :], start=(k == 0), stop=(k == H1 // P - 1))
                        last.then_inc(s_h2, 1)
                    if c == 1 and prev2:
                        pe.wait_ge(s_h2t, t - 1)
                        for k in range(H2 // P):
                            last = pe.matmul(p_o[0:1, 0:TILE], F("w3")[:, k:k + 1], h2_t[:, k, :],
                                             start=(k == 0), stop=(k == H2 // P - 1))
                        last.then_inc(s_o, 1)
                    if c == 3 and prev:
                        if known == 1:
                            pe.wait_ge(s_wls, QB)
                        pe.wait_ge(s_zk[o], ((t - 1 - o) // 2 + 1 if known is not None else uses + (1 - o)) * (16 * MOVES))
                        need(pe, s_osb, t - 1)
                        layer(o, range(0, 5))
                    if c == 4 and prev:
                        layer(o, range(5, ZK))
                    if c >= 4 and nxt:
                        nuses = uses + b
                        transposes(t + 1, o, c - 4, nuses)
                    if c == 6 and prev:
                        pe.wait_ge(s_zn, t)
                        for k in range(UK):
                            last = pe.transpose(p_o[:, k * TILE:(k + 1) * TILE], zn[:, k * P:(k + 1) * P], F("ident"))
                        last.then_inc(s_zt, 1)
                    if c == 7 and prev:
                        pe.wait_ge(s_znt, t * UK)
                        for m in range(H1 // P):
                            for k in range(UK + DK):
                                rhs = zn_t[:, k, :] if k < UK else dense_sb[:, k - UK, bass.ds((t - 1) * TILE, TILE)]
                                last = pe.matmul(p_o[:, m * TILE:(m + 1) * TILE], w1_sb[:, k, m * P:(m + 1) * P],
                                                 rhs, start=(k == 0), stop=(k == UK + DK - 1))
                        last.then_inc(s_h1, 1)

            over_tiles(pe, tile)

        @block.scalar
        def _(act):
            act.wait_ge(s_clear, 1)
            act.wait_ge(s_xmv, TILES)
            act.activation(x_sd[:, :], x_mv[:, :, 1], ACT.Sqrt, bias=eps_sb[:, 0:1]).then_inc(s_xsd, 1)
            xbanks = [p_z[0], p_z[1], p_y[0], p_y[1]]
            for q in range(4):
                act.wait_ge(s_xtr, q + 1)
                act.activation(x_t[:, 512 * q:512 * q + 512], xbanks[q][:, :], ACT.Identity,
                               scale=F("gd"), bias=F("bd")).then_inc(s_xt, 1)
            for q in range(4):
                act.wait_ge(s_xsmm, q + 1)
                act.activation(x_sum[64:96, 512 * q:512 * q + 512], p_u[q % 2][64:96, :],
                               ACT.Copy).then_inc(s_xs, 1)

            def land(t, k, b):
                need(act, s_tr, t * len(PIECES) + k + 1)
                a, z = PIECES[k]
                src = p_t[:, 0:(z - a) * TILE].rearrange("p (n b) -> p n b", n=z - a)
                for h in range(2):
                    dst = emb_t[b][64 * h:64 * h + 64, :, 2 * a + h:2 * z:2].rearrange("p b n -> p n b")
                    act.activation(dst, src[64 * h:64 * h + 64, :, :], ACT.Copy).then_inc(s_embt, 1)

            act.wait_ge(s_clear, 5)
            for k in range(len(PIECES)):
                land(0, k, 0)

            def tile(t, known, uses, b=None):
                live = known is None or known < TILES
                nxt = known is None or known + 1 < TILES
                prev = known is None or 1 <= known <= TILES
                b = known % 2 if b is None else b
                o = 1 - b
                for c in range(CHUNKS):
                    s = t * CHUNKS + c
                    q = c % 2
                    r = (c - 1) % 2
                    u_live = live and known != 0 or c == 0 and prev or known == 0 and c >= 1
                    z_live = live and known != 0 or c < 2 and prev or known == 0 and c >= 2
                    if live:
                        need(act, s_y, s + 1)
                        need(act, s_ssy, s - 1)
                        act.activation(sq_y[q][0:ROWS, :], p_y[q][0:ROWS, :], ACT.Square).then_inc(s_sqy, 1)
                    if u_live:
                        need(act, s_u, s)
                        need(act, s_ssu, s - 2)
                        act.activation(sq_u[r][:, :], p_u[r][:, :], ACT.Square).then_inc(s_squ, 1)
                    if live:
                        need(act, s_ssy, s + 1)
                        need(act, s_rsy, s - 1)
                        act.activation(sd_y[q][0:ROWS, :], ss_y[q][0:ROWS, :], ACT.Sqrt, scale=1.0 / E,
                                       bias=eps_sb[0:ROWS, 0:1]).then_inc(s_sdy, 1)
                    if z_live:
                        zb = b if c >= 2 else o
                        zc = (c - 2) % CHUNKS
                        need(act, s_z, s - 1)
                        if zc == 0:
                            need(act, s_zk[zb], uses * (16 * MOVES))
                        src = p_z[q][:, 0:GROUP * COLS].rearrange("p (i q) -> p i q", i=GROUP)
                        act.activation(
                            z_stage[zb][:, :, zc * GROUP:(zc + 1) * GROUP, :].rearrange("p j i q -> p i j q"),
                            src[:, :, 0:PROJ].rearrange("p i (j q) -> p i j q", j=4), ACT.Copy)
                        act.activation(
                            z_extra[zb][:, :, zc * GROUP:(zc + 1) * GROUP].rearrange("p e i -> p i e"),
                            src[:, :, PROJ:COLS], ACT.Copy).then_inc(s_zs, 1)
                    if u_live:
                        need(act, s_ssu, s)
                        need(act, s_rsu, s - 2)
                        act.activation(sd_u[r][:, :], ss_u[r][:, :], ACT.Sqrt, scale=1.0 / PROJ,
                                       bias=eps_sb[:, 0:1]).then_inc(s_sdu, 1)
                    if c >= 4 and nxt:
                        land(t + 1, c - 4, o)
                    if c == 5 and prev:
                        act.wait_ge(s_lmv, t)
                        act.activation(l_sd[:, :], l_mv[:, 1:2], ACT.Sqrt, bias=eps_sb[:, 0:1]).then_inc(s_lsd, 1)
                    if c == 6 and prev:
                        act.wait_ge(s_zt, t)
                        need(act, s_h1, t - 1)
                        for k in range(UK):
                            act.activation(zn_t[:, k, :], p_o[:, k * TILE:(k + 1) * TILE], ACT.Identity,
                                           scale=F("gl")[:, k:k + 1], bias=F("bl")[:, k:k + 1]).then_inc(s_znt, 1)
                    if c == 7 and prev:
                        act.wait_ge(s_h1, t)
                        need(act, s_h2, t - 1)
                        for m in range(H1 // P):
                            act.activation(h1_t[:, m, :], p_o[:, m * TILE:(m + 1) * TILE], ACT.Relu,
                                           bias=F("b1")[:, m:m + 1]).then_inc(s_h1t, 1)

            over_tiles(act, tile)

        @block.vector
        def _(v):
            v.memset(ones[:, :], 1.0)
            v.memset(eps_sb[:, :], EPS).then_inc(s_clear, 1)
            v.wait_ge(s_par, 16)
            v.tensor_reduce(means[:, 0:1], F("ws"), AX.X, ALU.add).then_inc(s_mean, 1)
            wsi3 = F("wsi").rearrange("p (g q) -> p g q", g=GROUP)
            v.tensor_reduce(means[:, 2:6], wsi3, AX.X, ALU.add).then_inc(s_mean, 1)
            v.wait_ge(s_mean, 2)
            v.tensor_scalar(means[:, 0:1], means[:, 0:1], 1.0 / E, None, ALU.mult).then_inc(s_mean, 1)
            v.tensor_scalar(means[:, 2:6], means[:, 2:6], 1.0 / PROJ, None, ALU.mult).then_inc(s_mean, 1)
            v.wait_ge(s_mean, 4)
            v.tensor_scalar(ws_c[:, :], F("ws"), means[:, 0:1], None, ALU.subtract).then_inc(s_cen, 1)
            v.tensor_tensor(wsi_c[:, :].rearrange("p (g q) -> p g q", g=GROUP), wsi3,
                            means[:, 2:6].unsqueeze(2).to_broadcast([P, GROUP, PROJ]), ALU.subtract).then_inc(s_cen, 1)
            v.memset(fold[:, :, :], 0.0).then_inc(s_fold, 1)
            v.wait_ge(s_fold, 1)
            S = fold[:, 0:QB, 32:64]
            v.tensor_tensor(S, F("delta_p").unsqueeze(1).to_broadcast([P, QB, PROJ]),
                            F("bsi_q").unsqueeze(2).to_broadcast([P, QB, PROJ]), ALU.mult).then_inc(s_fold, 1)
            v.tensor_scalar(fold[:, 0:QB, 96], F("bsi_q"), F("bsi_p"), float(E), ALU.mult, ALU.mult)
            v.tensor_scalar(fold[:, QB, 0:32], F("delta_p"), F("gsi_p"), None, ALU.mult)
            v.tensor_copy(fold[:, QB, 64:65], F("bsi_p")).then_inc(s_fold, 1)
            v.wait_ge(s_fold, 3)
            v.scalar_tensor_tensor(S, F("delta_q").rearrange("p (k q) -> p k q", k=QB), F("bsi_p"), S,
                                   ALU.mult, ALU.add).then_inc(s_fold, 1)
            v.wait_ge(s_fold, 4)
            v.tensor_tensor(S, S, F("gsi_free").unsqueeze(1).to_broadcast([P, QB, PROJ]), ALU.mult).then_inc(s_fold, 1)
            v.tensor_scalar(gg[:, :], F("gsi_q"), F("gsi_p"), None, ALU.mult).then_inc(s_fold, 1)
            banks = [p_y[0], p_y[1], p_u[0], p_u[1]]
            for t in range(TILES):
                if t % 4 == 0:
                    v.wait_ge(s_xmm, t // 4 + 1)
                v.bn_stats(x_stats[:, t, :], banks[t // 4][:, t % 4 * E:t % 4 * E + E]).then_inc(s_xstat, 1)
            for t in range(TILES):
                v.wait_ge(s_xstat, t + 1)
                v.bn_aggr(x_mv[:, t, :], x_stats[:, t, :]).then_inc(s_xmv, 1)
            v.wait_ge(s_xsd, 1)
            v.reciprocal(x_rs[:, :], x_sd[:, :]).then_inc(s_xrs, 1)
            v.wait_ge(s_xrs, 1)
            for t in range(TILES):
                v.tensor_scalar(xn[:, t, :], banks[t // 4][:, t % 4 * E:t % 4 * E + E], x_mv[:, t, 0:1],
                                x_rs[:, t:t + 1], ALU.subtract, ALU.mult).then_inc(s_xn, 1)
            for b in range(2):
                v.memset(emb_t[b][:, :, :], 0.0).then_inc(s_clear, 1)
                v.memset(z_9[b][:, :, :], 1.0).then_inc(s_clear, 1)
            v.wait_ge(s_wsimm, 1)
            v.wait_ge(s_cen, 2)
            v.tensor_copy(wsi_c[:, :], p_o[:, 0:P]).then_inc(s_wsi, 1)
            v.wait_ge(s_w9mm, 1)
            v.tensor_copy(w9[:, :], p_t[:, :]).then_inc(s_w9, 1)
            for k in range(QB):
                v.tensor_scalar(wl_sb[:, k, :], wl_sb[:, k, :], gg[:, k:k + 1], None, ALU.mult).then_inc(s_wls, 1)
            v.wait_ge(s_xtr, 4)
            for b in range(2):
                v.memset(feat[b][:, :, PROJ + 1], 1.0)

            def tile(t, known, uses, b=None):
                live = known is None or known < TILES
                prev = known is None or 1 <= known <= TILES
                prev2 = known is None or known >= 2
                b = known % 2 if b is None else b
                o = 1 - b
                for c in range(CHUNKS):
                    s = t * CHUNKS + c
                    q = c % 2
                    r = (c - 1) % 2
                    u_live = live and known != 0 or c == 0 and prev or known == 0 and c >= 1
                    if live:
                        need(v, s_sqy, s + 1)
                        v.tensor_reduce(ss_y[q][0:ROWS, :],
                                        sq_y[q][0:ROWS, :].rearrange("p (g e) -> p g e", g=4),
                                        AX.X, ALU.add).then_inc(s_ssy, 1)
                    if c == 5 and prev:
                        v.wait_ge(s_l, t)
                        v.bn_stats(l_stats[:, :], p_o[:, :]).then_inc(s_lst, 1)
                    if u_live:
                        if c == 5 and prev:
                            v.wait_ge(s_lst, t)
                        need(v, s_squ, s)
                        v.tensor_reduce(ss_u[r][:, :], sq_u[r][:, :].rearrange("p (b q) -> p b q", b=CHUNK),
                                        AX.X, ALU.add).then_inc(s_ssu, 1)
                    if c == 5 and prev:
                        if not u_live:
                            v.wait_ge(s_lst, t)
                        v.bn_aggr(l_mv[:, :], l_stats[:, :]).then_inc(s_lmv, 1)
                    if live:
                        need(v, s_sdy, s + 1)
                        v.reciprocal(rs_y[q][0:ROWS, :], sd_y[q][0:ROWS, :]).then_inc(s_rsy, 1)
                        need(v, s_rsy, s + 1)
                        need(v, s_u, s - 1)
                        for g in range(4):
                            last = v.scalar_tensor_tensor(
                                y_sb[q][0:ROWS, g, :], p_y[q][0:ROWS, g * E:g * E + E], rs_y[q][0:ROWS, g:g + 1],
                                F("gs", 0, ROWS), ALU.mult, ALU.mult)
                        last.then_inc(s_ysb, 1)
                    if u_live:
                        fc = (c - 1) % CHUNKS
                        fb = b if c >= 1 else o
                        need(v, s_sdu, s)
                        v.reciprocal(rs_u[r][:, :], sd_u[r][:, :]).then_inc(s_rsu, 1)
                        if fc == 0:
                            need(v, s_z, (t - 1) * CHUNKS)
                            if known == 0:
                                v.wait_ge(s_xt, 4)
                            v.tensor_copy(feat[fb][:, :, PROJ], x_t[:, bass.ds(t * TILE, TILE)])
                        need(v, s_rsu, s)
                        dst = feat[fb][:, :, 0:PROJ].rearrange("p (g c i) q -> p g c i q", g=4, i=GROUP)
                        v.tensor_tensor(dst[:, :, fc, :, :],
                                        p_u[r][:, :].rearrange("p (g i q) -> p g i q", g=4, i=GROUP),
                                        rs_u[r][:, :].rearrange("p (g i) -> p g i", g=4).unsqueeze(3)
                                        .to_broadcast([P, 4, GROUP, PROJ]), ALU.mult).then_inc(s_feat, 1)
                    if c == 5 and prev:
                        v.wait_ge(s_lsd, t)
                        v.reciprocal(l_rs[:, :], l_sd[:, :]).then_inc(s_lrs, 1)
                        v.wait_ge(s_lrs, t)
                        v.tensor_scalar(zn[:, :], p_o[:, 0:USED], l_mv[:, 0:1], l_rs[:, 0:1],
                                        ALU.subtract, ALU.mult).then_inc(s_zn, 1)
                    if c == 0 and prev2:
                        v.wait_ge(s_h2, t - 1)
                        for m in range(H2 // P):
                            last = v.tensor_scalar(h2_t[:, m, :], p_o[:, m * TILE:(m + 1) * TILE],
                                                   F("b2")[:, m:m + 1], 0.0, ALU.add, ALU.max)
                        last.then_inc(s_h2t, 1)
                    if c == 1 and prev2:
                        v.wait_ge(s_o, t - 1)
                        v.tensor_copy(out_sb[0:1, bass.ds((t - 2) * TILE, TILE)], p_o[0:1, 0:TILE]).then_inc(s_osb, 1)

            over_tiles(v, tile)


def kernel(**inputs):
    import concourse.bacc as _bacc
    from concourse.bass_utils import run_bass_kernel_spmd as _run

    a = {name: np.ascontiguousarray(value) for name, value in inputs.items()}
    f32 = np.float32

    tri = {(i, j): i * (i - 1) // 2 + j for i in range(PROJ + 1) for j in range(i)}
    wlT = a["L0_rec_Wl"].T
    wl = np.zeros((P, ZK, MAXD), f32)
    for p in range(PROJ):
        wl[p, QB] = wlT[tri[p + 1, 0]]
        for q in range(p):
            wl[PROJ * (q // QB) + p, q % QB] = wlT[tri[p + 1, q + 1]]

    prm = np.zeros((P, NPAR), f32)

    def put(name, value, rows=slice(None)):
        lo, hi = FIELD[name]
        prm[rows, lo:hi] = value

    put("ident", np.eye(P, dtype=f32))
    isum = np.zeros((P, P), f32)
    isum[:ROWS, :ROWS] = np.eye(ROWS, dtype=f32)
    isum[:ROWS, ROWS] = 1.0
    put("ident_sum", isum)
    put("delta_p", np.tile(np.eye(PROJ, dtype=f32), (4, 1)))
    dq = np.zeros((P, QB, PROJ), f32)
    bq = np.zeros((P, QB), f32)
    gq = np.zeros((P, QB), f32)
    gsi, bsi = a["L0_rec_gsi"], a["L0_rec_bsi"]
    for j in range(4):
        for k in range(QB):
            dq[PROJ * j:PROJ * j + PROJ, k, QB * j + k] = 1.0
            bq[PROJ * j:PROJ * j + PROJ, k] = bsi[QB * j + k]
            gq[PROJ * j:PROJ * j + PROJ, k] = gsi[QB * j + k]
    put("delta_q", dq.reshape(P, QB * PROJ))
    put("bsi_q", bq)
    put("gsi_q", gq)
    put("bsi_p", np.tile(bsi, 4)[:, None])
    put("gsi_p", np.tile(gsi, 4)[:, None])
    put("gsi_free", np.tile(gsi, (P, 1)))
    put("ws", np.concatenate([a["L0_rec_Ws"].T, a["L0_rec_Ws"].T]))
    wsi = np.zeros((P, P), f32)
    for g in range(GROUP):
        wsi[NF * g:NF * g + NF, PROJ * g:PROJ * g + PROJ] = a["L0_rec_Wsi"].T
    put("wsi", wsi)
    put("gs", np.tile(a["L0_rec_gs"], (P, 1)))
    put("gd", a["L0_rec_gd"][:, None])
    put("bd", a["L0_rec_bd"][:, None])
    put("gl", a["L0_rec_gl"][:USED].reshape(UK, P).T)
    put("bl", a["L0_rec_bl"][:USED].reshape(UK, P).T)
    put("b1", a["b_top1"].reshape(H1 // P, P).T)
    put("b2", a["b_top2"].reshape(H2 // P, P).T)
    put("w3", a["W_top3"].reshape(H2 // P, P).T)
    put("wd", a["L0_rec_Wd"].T.reshape(DK, P, E).transpose(1, 0, 2).reshape(P, DK * E))

    nc = _bacc.Bacc("TRN2", target_bir_lowering=False, num_devices=1)
    arrays = {f"tbl_{n}_dram": a[f"tbl_{n}"] for n in range(NF)}
    arrays.update(
        ids_dram=a["ids"], params_dram=prm,
        bs_dram=np.tile(a["L0_rec_bs"], (1, 4)).reshape(1, 4, E),
        dense_dram=np.ascontiguousarray(a["r_dense_t"].T), wl_dram=wl,
        w1_dram=a["W_top1"], w2_dram=a["W_top2"])
    ap = {k: nc.dram_tensor(k, x.shape, mybir.dt.from_np(x.dtype), kind="ExternalInput").ap()
          for k, x in arrays.items()}
    out = nc.dram_tensor("out_dram", (BATCH, 1), mybir.dt.float32, kind="ExternalOutput").ap()
    build(nc, [ap[f"tbl_{n}_dram"] for n in range(NF)], ap["ids_dram"], ap["params_dram"], ap["bs_dram"],
          ap["dense_dram"], ap["wl_dram"], ap["w1_dram"], ap["w2_dram"], out)
    r = _run(nc, [arrays], core_ids=[0])
    return r.results[0]["out_dram"]
```

```python
import concourse.bass as bass
import numpy as np
from concourse import mybir
from contextlib import ExitStack

BATCH = 2048
NF = 26
DSP = 64
E = 128
PROJ = 32
DD = 256
MAXD = 512
USED = 384
H1, H2 = 512, 256
EPS = 1e-5

P = 128
TILE = 128
TILES = BATCH // TILE
GROUP = 4
CHUNK = 4 * GROUP
CHUNKS = TILE // CHUNK
ROWS = GROUP * NF
ZK = 6
BLOCKS = [(q, PROJ - 1 - q) for q in range(0, PROJ - ZK + 1, ZK)]
REST_AT = sum(n for _, n in BLOCKS)
REST_Q = ZK * len(BLOCKS)
COLS = REST_Q + ZK
X_AT, ONE_AT = PROJ, PROJ + 1
SUM_STEP, ONE_STEP = ONE_AT - REST_Q, ONE_AT - REST_Q + 1
WCUT = 64
assert REST_AT + PROJ == P - 1 and REST_Q == PROJ - 2 and REST_AT >= WCUT and ONE_STEP < ZK
UK = USED // P
DK = DD // P
PIECES = [(0, 4), (4, 7), (7, 10), (10, 13)]
SLOTS = TILE // 4
MOVES = len(BLOCKS) + 2

_FIELDS = [("ident", P), ("ident_sum", P), ("delta_p", ZK * PROJ), ("delta_q", ZK * PROJ), ("bsi_p", ZK),
           ("bsi_q", ZK), ("bsi_x", ZK), ("gsi_p", ZK), ("gsi_q", ZK), ("gsi_free", PROJ), ("ws", E), ("wsi", P),
           ("gs", E), ("gd", 1), ("bd", 1), ("gl", UK), ("bl", UK), ("b1", H1 // P), ("b2", H2 // P),
           ("w3", H2 // P), ("wd", DK * E)]
FIELD = {}
NPAR = 0
for _name, _width in _FIELDS:
    FIELD[_name] = (NPAR, NPAR + _width)
    NPAR += _width


def build(nc, tables, ids, params, bs_row, dense_t, wl, w1, w2, out):
    fp32 = mybir.dt.float32
    i32 = mybir.dt.int32
    ALU = mybir.AluOpType
    ACT = mybir.ActivationFunctionType
    AX = mybir.AxisListType

    with ExitStack() as ctx:
        def sb(name, shape, dt=fp32):
            return ctx.enter_context(nc.sbuf_tensor(name, shape, dt))

        def bank(name):
            return ctx.enter_context(nc.psum_tensor(name, [P, 512], fp32))

        def sem(name):
            return ctx.enter_context(nc.semaphore(name))

        par = sb("par", [P, NPAR])
        wl_sb = sb("wl_sb", [P, ZK, MAXD])
        w1_sb = sb("w1_sb", [P, UK + DK, H1])
        w2_sb = sb("w2_sb", [P, H1 // P, H2])
        dense_sb = sb("dense_sb", [P, DK, BATCH])
        fold = sb("fold", [P, 2, ZK, P - WCUT])
        ws_c = sb("ws_c", [P, E])
        wsi_c = sb("wsi_c", [P, P])
        gg = sb("gg", [P, ZK])
        pair_sum = sb("pair_sum", [P, ZK, PROJ])
        pair_q = sb("pair_q", [P, ZK, PROJ])
        means = sb("means", [P, 8])
        ones = sb("ones", [P, 1])
        eps_sb = sb("eps_sb", [P, 1])
        x_stats = sb("x_stats", [P, TILES, 6])
        x_mv = sb("x_mv", [P, TILES, 2])
        x_sd = sb("x_sd", [P, TILES])
        x_rs = sb("x_rs", [P, TILES])
        x_t = sb("x_t", [P, BATCH])
        x_sum = sb("x_sum", [P, TILES, ZK])
        sum_dram = nc.dram_tensor("sum_dram", (TILES, TILE, ZK), fp32).ap()

        idx = [sb(f"idx{i}", [P, NF], i32) for i in range(2)]
        emb = [sb(f"emb{i}", [P, NF, DSP]) for i in range(2)]
        emb_t = [sb(f"emb_t{i}", [P, TILE, NF]) for i in range(2)]
        feat = [sb(f"feat{i}", [P, TILE, COLS]) for i in range(2)]
        sq_y = [sb(f"sq_y{i}", [P, 512]) for i in range(2)]
        ss_y = [sb(f"ss_y{i}", [P, 4]) for i in range(2)]
        sd_y = [sb(f"sd_y{i}", [P, 4]) for i in range(2)]
        rs_y = [sb(f"rs_y{i}", [P, 4]) for i in range(2)]
        y_sb = [sb(f"y_sb{i}", [P, 4, E]) for i in range(2)]
        sq_u = [sb(f"sq_u{i}", [P, 512]) for i in range(2)]
        ss_u = [sb(f"ss_u{i}", [P, CHUNK]) for i in range(2)]
        sd_u = [sb(f"sd_u{i}", [P, CHUNK]) for i in range(2)]
        rs_u = [sb(f"rs_u{i}", [P, CHUNK]) for i in range(2)]
        z_stage = [sb(f"z_stage{i}", [P, COLS // ZK, SLOTS, ZK]) for i in range(2)]
        z_k = [sb(f"z_k{i}", [P, 4, SLOTS, ZK]) for i in range(2)]
        z_dram = [nc.dram_tensor(f"z_dram{i}", (4, PROJ, COLS // ZK, SLOTS * ZK), fp32).ap() for i in range(2)]
        zn = sb("zn", [P, USED])
        l_stats = sb("l_stats", [P, 6])
        l_mv = sb("l_mv", [P, 2])
        l_sd = sb("l_sd", [P, 1])
        l_rs = sb("l_rs", [P, 1])
        zn_t = sb("zn_t", [P, UK, TILE])
        h1_t = sb("h1_t", [P, H1 // P, TILE])
        h2_t = sb("h2_t", [P, H2 // P, TILE])
        out_sb = sb("out_sb", [1, BATCH])
        xn = feat[0][:, :, :].rearrange("p a b -> p (a b)")[:, 0:BATCH].rearrange("p (t e) -> p t e", t=TILES)

        p_y = [bank(f"p_y{i}") for i in range(2)]
        p_u = [bank(f"p_u{i}") for i in range(2)]
        p_z = [bank(f"p_z{i}") for i in range(2)]
        p_t = bank("p_t")
        p_o = bank("p_o")

        def F(name, lo=0, hi=P):
            a, b = FIELD[name]
            return par[lo:hi, a:b]

        s_par = sem("s_par")
        s_dense = sem("s_dense")
        s_wl = sem("s_wl")
        s_w12 = sem("s_w12")
        s_bsrow = sem("s_bsrow")
        s_idx = [sem(f"s_idx{i}") for i in range(2)]
        s_gather = [sem(f"s_gather{i}") for i in range(2)]
        s_start = sem("s_start")
        s_clear = sem("s_clear")
        s_xmm = sem("s_xmm")
        s_xstat = sem("s_xstat")
        s_xmv = sem("s_xmv")
        s_xsd = sem("s_xsd")
        s_xrs = sem("s_xrs")
        s_xn = sem("s_xn")
        s_xtr = sem("s_xtr")
        s_xt = sem("s_xt")
        s_xsmm = sem("s_xsmm")
        s_xs = sem("s_xs")
        s_sumd = sem("s_sumd")
        s_mean = sem("s_mean")
        s_cen = sem("s_cen")
        s_wsimm = sem("s_wsimm")
        s_wsi = sem("s_wsi")
        s_fold = sem("s_fold")
        s_foldmm = sem("s_foldmm")
        s_wls = sem("s_wls")
        s_y = sem("s_y")
        s_sqy = sem("s_sqy")
        s_ssy = sem("s_ssy")
        s_sdy = sem("s_sdy")
        s_rsy = sem("s_rsy")
        s_ysb = sem("s_ysb")
        s_u = sem("s_u")
        s_squ = sem("s_squ")
        s_ssu = sem("s_ssu")
        s_sdu = sem("s_sdu")
        s_rsu = sem("s_rsu")
        s_feat = sem("s_feat")
        s_z = sem("s_z")
        s_zs = sem("s_zs")
        s_tr = sem("s_tr")
        s_embt = sem("s_embt")
        s_zd = sem("s_zd")
        s_zk = [sem(f"s_zk{i}") for i in range(2)]
        s_l = sem("s_l")
        s_lst = sem("s_lst")
        s_lmv = sem("s_lmv")
        s_lsd = sem("s_lsd")
        s_lrs = sem("s_lrs")
        s_zn = sem("s_zn")
        s_zt = sem("s_zt")
        s_znt = sem("s_znt")
        s_h1 = sem("s_h1")
        s_h1t = sem("s_h1t")
        s_h2 = sem("s_h2")
        s_h2t = sem("s_h2t")
        s_o = sem("s_o")
        s_osb = sem("s_osb")
        s_out = sem("s_out")

        block = ctx.enter_context(nc.Block())

        def need(eng, s, value):
            if not isinstance(value, int) or value > 0:
                eng.wait_ge(s, value)

        def over_tiles(eng, tile):
            for t in (0, 1):
                tile(t, t, 0)
            with eng.Fori(1, TILES // 2 - 1) as i:
                for par_ in range(2):
                    tile(i * 2 + par_, None, i, par_)
            for t in range(TILES - 2, TILES + 2):
                tile(t, t, t // 2)

        COMBINE, NORM, INTERACT = 1, 2, 3

        def piece_chunk(known):
            return 4 if known == 0 else 3

        def there(known, c, lag=0):
            return known is None or 0 <= known * CHUNKS + c - lag < TILES * CHUNKS

        @block.sync
        def _(sp):
            sp.dma_start(idx[0][:, :], ids[0:TILE, :]).then_inc(s_idx[0], 16)
            sp.dma_start(par[:, :], params).then_inc(s_par, 16)
            sp.dma_start(idx[1][:, :], ids[TILE:2 * TILE, :]).then_inc(s_idx[1], 16)
            sp.dma_start(dense_sb[:, :, :], dense_t.rearrange("(k p) b -> p k b", p=P)).then_inc(s_dense, 16)
            sp.dma_start(wl_sb[:, :, :], wl).then_inc(s_wl, 16)
            for b in range(2):
                sp.dma_start(y_sb[b][ROWS:ROWS + 1, :, :], bs_row).then_inc(s_bsrow, 16)
            sp.dma_start(w1_sb[:, 0:UK, :],
                         w1[0:USED, :].rearrange("(k p) n -> p k n", p=P)).then_inc(s_w12, 16)
            sp.dma_start(w1_sb[:, UK:UK + DK, :],
                         w1[MAXD:MAXD + DD, :].rearrange("(k p) n -> p k n", p=P)).then_inc(s_w12, 16)
            sp.dma_start(w2_sb[:, :, :], w2.rearrange("(k p) n -> p k n", p=P)).then_inc(s_w12, 16)
            sp.wait_ge(s_xs, 1)
            sp.dma_start(sum_dram.rearrange("t b k -> b t k"), x_sum[:, :, :]).then_inc(s_sumd, 16)
            sp.wait_ge(s_sumd, 16)
            sums = sum_dram.rearrange("t b k -> t (b k)")

            def held(value):
                return value if isinstance(value, int) else sp.snap(value)

            def tile(t, known, uses, b=None):
                b = known % 2 if b is None else b
                if known is None or known + 2 < TILES:
                    row, gathered = held((t + 2) * TILE), held((uses + 1) * (16 * NF))
                    sp.wait_ge(s_gather[b], gathered)
                    sp.dma_start(idx[b][:, :], ids[bass.ds(row, TILE), :]).then_inc(s_idx[b], 16)
                if known is None or 1 <= known <= TILES:
                    o = 1 - b
                    staged, row = held(t * CHUNKS), held(t - 1)
                    need(sp, s_zs, staged)
                    sp.dma_start(z_dram[o].rearrange("g p j n -> (g p) (j n)"),
                                 z_stage[o][:, :, :, :].rearrange("p j i q -> p (j i q)")).then_inc(s_zd, 16)
                    sp.wait_ge(s_zd, t * 16)
                    src = z_dram[o].rearrange("g p j n -> p j g n")
                    dst = z_k[o][:, :, :, :].rearrange("p g i q -> p g (i q)")
                    at = 0
                    for j, (q, n) in enumerate(BLOCKS):
                        sp.dma_start(dst[at:at + n, :, :], src[q + 1:q + 1 + n, j, :, :]).then_inc(s_zk[o], 16)
                        at += n
                    sp.dma_start(dst[at:at + PROJ, :, :], src[:, len(BLOCKS), :, :]).then_inc(s_zk[o], 16)
                    sp.dma_start(dst[P - 1:P, :, :].rearrange("p g n -> p (g n)"),
                                 sums[bass.ds(row, 1), :]).then_inc(s_zk[o], 16)

            over_tiles(sp, tile)
            sp.wait_ge(s_osb, TILES)
            sp.dma_start(out.rearrange("b a -> a b"), out_sb[:, :]).then_inc(s_out, 16)
            sp.wait_ge(s_out, 16)

        @block.gpsimd
        def _(pool):
            def tile(t, known, uses, b=None):
                if known is not None and known >= TILES:
                    return
                b = known % 2 if b is None else b
                pool.wait_ge(s_idx[b], (uses + 1) * 16)
                need(pool, s_tr, (t - 1) * len(PIECES))
                pool.sem_inc(s_start, 1)
                for n in range(NF):
                    pool.indirect_dma_start(
                        emb[b][:, n, :], None, tables[n],
                        bass.IndirectOffsetOnAxis(ap=idx[b][:, n:n + 1], axis=0)).then_inc(s_gather[b], 16)

            over_tiles(pool, tile)

        @block.tensor
        def _(pe):
            banks = [p_y[0], p_y[1], p_u[0], p_u[1]]
            pe.wait_ge(s_par, 16)
            pe.wait_ge(s_dense, 16)
            wd = F("wd").rearrange("p (k e) -> p k e", k=DK)
            for q in range(4):
                for i in range(4):
                    t = 4 * q + i
                    for k in range(DK):
                        last = pe.matmul(banks[q][:, i * E:i * E + E], dense_sb[:, k, t * TILE:t * TILE + TILE],
                                         wd[:, k, :], start=(k == 0), stop=(k == DK - 1))
                last.then_inc(s_xmm, 1)
            pe.wait_ge(s_cen, 2)
            pe.matmul(p_o[:, 0:P], F("ident_sum", 0, ROWS), wsi_c[0:ROWS, :], start=True, stop=True).then_inc(s_wsimm, 1)
            pe.wait_ge(s_wl, 16)
            pe.wait_ge(s_fold, 7)
            for m, dst in enumerate([p_t, p_z[0]]):
                for k in range(ZK):
                    last = pe.matmul(dst[WCUT:P, :], fold[:, m, k, :], wl_sb[:, k, :],
                                     start=(k == 0), stop=(k == ZK - 1))
            last.then_inc(s_foldmm, 1)
            xbanks = [p_y[0], p_y[1], p_u[0], p_u[1]]
            pe.wait_ge(s_xn, TILES)
            for q in range(4):
                for i in range(4):
                    last = pe.transpose(xbanks[q][:, i * TILE:i * TILE + TILE], xn[:, 4 * q + i, :], F("ident"))
                last.then_inc(s_xtr, 1)
            pe.wait_ge(s_clear, 1)
            pe.wait_ge(s_wsi, 1)
            pe.wait_ge(s_xt, 4)
            for t in range(TILES):
                last = pe.matmul(p_o[:, t:t + 1], x_t[:, t * TILE:(t + 1) * TILE], ones[:, :], start=True, stop=True)
            last.then_inc(s_xsmm, 1)

            def transposes(t, b, k, uses):
                if k == 0:
                    pe.wait_ge(s_gather[b], (uses + 1) * (16 * NF))
                need(pe, s_embt, (t * len(PIECES) + k) * 2)
                a, z = PIECES[k]
                for n in range(a, z):
                    last = pe.transpose(p_t[:, (n - a) * TILE:(n - a + 1) * TILE],
                                        emb[b][:, 2 * n:2 * n + 2, :].rearrange("p n d -> p (n d)"), F("ident"))
                last.then_inc(s_tr, 1)

            pe.wait_ge(s_wls, ZK)
            for k in range(len(PIECES)):
                transposes(0, 0, k, 0)
            pe.wait_ge(s_bsrow, 32)
            pe.wait_ge(s_w12, 48)

            def project(s, c, b):
                for g in range(4):
                    e0 = g * SLOTS + c * GROUP
                    last = pe.matmul(p_y[c % 2][0:ROWS, g * E:g * E + E],
                                     emb_t[b][:, e0:e0 + GROUP, :].rearrange("p a b -> p (a b)"),
                                     ws_c[:, :], start=True, stop=True)
                last.then_inc(s_y, 1)

            def combine(c):
                for g in range(4):
                    last = pe.matmul(p_u[c % 2][:, g * P:g * P + P], y_sb[c % 2][0:ROWS + 1, g, :],
                                     wsi_c[0:ROWS + 1, :], start=True, stop=True)
                last.then_inc(s_u, 1)

            def interact(c, b):
                for e in range(CHUNK):
                    i, g = e // 4, e % 4
                    v = feat[b][:, g * SLOTS + c * GROUP + i, :]
                    last = pe.matmul(p_z[c % 2][32 * g:32 * g + 32, i * COLS:(i + 1) * COLS],
                                     v[:, 0:PROJ], v, start=True, stop=True)
                last.then_inc(s_z, 1)

            def layer(b, ks):
                for k in ks:
                    last = pe.matmul(p_o[:, :], z_k[b][:, :, :, k].rearrange("p g i -> p (g i)"), wl_sb[:, k, :],
                                     start=(k == 0), stop=(k == ZK - 1))
                if ks[-1] == ZK - 1:
                    last.then_inc(s_l, 1)

            def tile(t, known, uses, b=None):
                live = known is None or known < TILES
                nxt = known is None or known + 1 < TILES
                prev = known is None or 1 <= known <= TILES
                prev2 = known is None or known >= 2
                b = known % 2 if b is None else b
                o = 1 - b
                for c in range(CHUNKS):
                    s = t * CHUNKS + c
                    if live:
                        if c == 0:
                            need(pe, s_embt, (t + 1) * (2 * len(PIECES)))
                        need(pe, s_ysb, s - 1)
                        project(s, c, b)
                    if there(known, c, INTERACT):
                        need(pe, s_feat, s - 2)
                        need(pe, s_zs, s - 4)
                        interact((c - INTERACT) % CHUNKS, b if c >= INTERACT else o)
                    if c == 0 and prev2:
                        layer(b, range(4, ZK))
                    if c == 2 and prev2:
                        pe.wait_ge(s_zn, t - 1)
                        need(pe, s_osb, t - 2)
                        for k in range(UK):
                            last = pe.transpose(p_t[:, k * TILE:(k + 1) * TILE], zn[:, k * P:(k + 1) * P], F("ident"))
                        last.then_inc(s_zt, 1)
                    if c in (3, 4) and prev2:
                        if c == 3:
                            pe.wait_ge(s_znt, (t - 1) * UK)
                        for m in range(2 * (c - 3), 2 * (c - 2)):
                            for k in range(UK + DK):
                                rhs = zn_t[:, k, :] if k < UK else dense_sb[:, k - UK, bass.ds((t - 2) * TILE, TILE)]
                                last = pe.matmul(p_o[:, m * TILE:(m + 1) * TILE], w1_sb[:, k, m * P:(m + 1) * P],
                                                 rhs, start=(k == 0), stop=(k == UK + DK - 1))
                        if c == 4:
                            last.then_inc(s_h1, 1)
                    if c == 5 and prev2:
                        pe.wait_ge(s_h1t, (t - 1) * (H1 // P))
                        for m in range(H2 // P):
                            for k in range(H1 // P):
                                last = pe.matmul(p_o[:, m * TILE:(m + 1) * TILE], w2_sb[:, k, m * P:(m + 1) * P],
                                                 h1_t[:, k, :], start=(k == 0), stop=(k == H1 // P - 1))
                        last.then_inc(s_h2, 1)
                    if c >= 6 and prev:
                        if c == 6:
                            spread = (known + 1) // 2 if known is not None else uses + b
                            pe.wait_ge(s_zk[o], spread * (16 * MOVES))
                            need(pe, s_h2t, t - 1)
                        layer(o, range(2 * (c - 6), 2 * (c - 5)))
                    k = c - piece_chunk(known)
                    if 0 <= k < len(PIECES) and nxt:
                        nuses = (known + 1) // 2 if known is not None else uses + b
                        transposes(t + 1, o, k, nuses)
                    if c == 7 and prev2:
                        pe.wait_ge(s_h2t, t - 1)
                        pe.wait_ge(s_embt, min(t + 2, TILES) * 2 * len(PIECES) if known is not None
                                   else (t + 2) * (2 * len(PIECES)))
                        for k in range(H2 // P):
                            last = pe.matmul(p_t[0:1, 0:TILE], F("w3")[:, k:k + 1], h2_t[:, k, :],
                                             start=(k == 0), stop=(k == H2 // P - 1))
                        last.then_inc(s_o, 1)
                    if there(known, c, COMBINE):
                        need(pe, s_ysb, s)
                        need(pe, s_feat, s - 2)
                        combine((c - COMBINE) % CHUNKS)

            over_tiles(pe, tile)

        @block.scalar
        def _(act):
            act.wait_ge(s_clear, 1)
            act.wait_ge(s_xmv, TILES)
            act.activation(x_sd[:, :], x_mv[:, :, 1], ACT.Sqrt, bias=eps_sb[:, 0:1]).then_inc(s_xsd, 1)
            xbanks = [p_y[0], p_y[1], p_u[0], p_u[1]]
            for q in range(4):
                act.wait_ge(s_xtr, q + 1)
                act.activation(x_t[:, 512 * q:512 * q + 512], xbanks[q][:, :], ACT.Identity,
                               scale=F("gd"), bias=F("bd")).then_inc(s_xt, 1)
            act.wait_ge(s_xsmm, 1)
            act.activation(x_sum[:, :, SUM_STEP], p_o[:, 0:TILES], ACT.Copy).then_inc(s_xs, 1)

            def land(t, k, b):
                need(act, s_tr, t * len(PIECES) + k + 1)
                a, z = PIECES[k]
                src = p_t[:, 0:(z - a) * TILE].rearrange("p (n b) -> p n b", n=z - a)
                for h in range(2):
                    dst = emb_t[b][64 * h:64 * h + 64, :, 2 * a + h:2 * z:2].rearrange("p b n -> p n b")
                    act.activation(dst, src[64 * h:64 * h + 64, :, :], ACT.Copy).then_inc(s_embt, 1)

            act.wait_ge(s_clear, 3)
            for k in range(len(PIECES)):
                land(0, k, 0)

            def tile(t, known, uses, b=None):
                live = known is None or known < TILES
                nxt = known is None or known + 1 < TILES
                prev = known is None or 1 <= known <= TILES
                prev2 = known is None or known >= 2
                b = known % 2 if b is None else b
                o = 1 - b
                for c in range(CHUNKS):
                    s = t * CHUNKS + c
                    q = c % 2
                    if there(known, c, NORM):
                        need(act, s_u, s - 1)
                        need(act, s_ssu, s - 3)
                        act.activation(sq_u[q][:, :], p_u[q][:, :], ACT.Square).then_inc(s_squ, 1)
                    if live:
                        need(act, s_y, s + 1)
                        need(act, s_ssy, s - 1)
                        act.activation(sq_y[q][0:ROWS, :], p_y[q][0:ROWS, :], ACT.Square).then_inc(s_sqy, 1)
                    if there(known, c, NORM):
                        need(act, s_ssu, s - 1)
                        need(act, s_rsu, s - 3)
                        act.activation(sd_u[q][:, :], ss_u[q][:, :], ACT.Sqrt, scale=1.0 / PROJ,
                                       bias=eps_sb[:, 0:1]).then_inc(s_sdu, 1)
                    if live:
                        need(act, s_ssy, s + 1)
                        need(act, s_rsy, s - 1)
                        act.activation(sd_y[q][0:ROWS, :], ss_y[q][0:ROWS, :], ACT.Sqrt, scale=1.0 / E,
                                       bias=eps_sb[0:ROWS, 0:1]).then_inc(s_sdy, 1)
                    if there(known, c, INTERACT):
                        zb = b if c >= INTERACT else o
                        zc = (c - INTERACT) % CHUNKS
                        need(act, s_z, s - 2)
                        if zc == 0:
                            need(act, s_zk[zb], uses * (16 * MOVES))
                        act.activation(
                            z_stage[zb][:, :, zc * GROUP:(zc + 1) * GROUP, :].rearrange("p j i q -> p i j q"),
                            p_z[1 - q][:, 0:GROUP * COLS].rearrange("p (i j q) -> p i j q", i=GROUP, q=ZK),
                            ACT.Copy).then_inc(s_zs, 1)
                    if c == 2 and prev2:
                        act.wait_ge(s_zt, t - 1)
                        need(act, s_h1, t - 2)
                        for k in range(UK):
                            act.activation(zn_t[:, k, :], p_t[:, k * TILE:(k + 1) * TILE], ACT.Identity,
                                           scale=F("gl")[:, k:k + 1], bias=F("bl")[:, k:k + 1]).then_inc(s_znt, 1)
                    if c == 4 and prev2:
                        act.wait_ge(s_h1, t - 1)
                        need(act, s_h2, t - 2)
                        for m in range(H1 // P):
                            act.activation(h1_t[:, m, :], p_o[:, m * TILE:(m + 1) * TILE], ACT.Relu,
                                           bias=F("b1")[:, m:m + 1]).then_inc(s_h1t, 1)
                    if c == 1 and prev2:
                        act.wait_ge(s_lmv, t - 1)
                        act.activation(l_sd[:, :], l_mv[:, 1:2], ACT.Sqrt, bias=eps_sb[:, 0:1]).then_inc(s_lsd, 1)
                    k = c - piece_chunk(known)
                    if 0 <= k < len(PIECES) and nxt:
                        land(t + 1, k, o)

            over_tiles(act, tile)

        @block.vector
        def _(v):
            v.memset(ones[:, :], 1.0)
            v.memset(x_sum[:, :, :], 1.0)
            v.memset(eps_sb[:, :], EPS).then_inc(s_clear, 1)
            v.wait_ge(s_par, 16)
            v.tensor_reduce(means[:, 0:1], F("ws"), AX.X, ALU.add).then_inc(s_mean, 1)
            wsi3 = F("wsi").rearrange("p (g q) -> p g q", g=GROUP)
            v.tensor_reduce(means[:, 2:6], wsi3, AX.X, ALU.add).then_inc(s_mean, 1)
            v.wait_ge(s_mean, 2)
            v.tensor_scalar(means[:, 0:1], means[:, 0:1], 1.0 / E, None, ALU.mult).then_inc(s_mean, 1)
            v.tensor_scalar(means[:, 2:6], means[:, 2:6], 1.0 / PROJ, None, ALU.mult).then_inc(s_mean, 1)
            v.wait_ge(s_mean, 4)
            v.tensor_scalar(ws_c[:, :], F("ws"), means[:, 0:1], None, ALU.subtract).then_inc(s_cen, 1)
            v.tensor_tensor(wsi_c[:, :].rearrange("p (g q) -> p g q", g=GROUP), wsi3,
                            means[:, 2:6].unsqueeze(2).to_broadcast([P, GROUP, PROJ]), ALU.subtract).then_inc(s_cen, 1)
            v.memset(fold[:, :, :, :], 0.0).then_inc(s_fold, 1)
            v.wait_ge(s_fold, 1)
            lo = REST_AT - WCUT
            S = pair_sum[:, :, :]
            v.tensor_tensor(S, F("delta_p").rearrange("p (k r) -> p k r", k=ZK),
                            F("bsi_q").unsqueeze(2).to_broadcast([P, ZK, PROJ]), ALU.mult).then_inc(s_fold, 1)
            v.tensor_tensor(pair_q[:, :, :], F("delta_q").rearrange("p (k r) -> p k r", k=ZK),
                            F("bsi_p").unsqueeze(2).to_broadcast([P, ZK, PROJ]), ALU.mult).then_inc(s_fold, 1)
            v.wait_ge(s_fold, 3)
            v.tensor_tensor(S, S, pair_q[:, :, :], ALU.add).then_inc(s_fold, 1)
            v.wait_ge(s_fold, 4)
            v.tensor_tensor(fold[:, 0, :, lo:lo + PROJ], S, F("gsi_free").unsqueeze(1).to_broadcast([P, ZK, PROJ]),
                            ALU.mult)
            v.tensor_copy(fold[:, 0, :, P - WCUT - 1], F("bsi_x")).then_inc(s_fold, 1)
            v.scalar_tensor_tensor(fold[:, 1, :, P - WCUT - 1], F("bsi_p"), float(E), F("bsi_q"),
                                   ALU.mult, ALU.mult).then_inc(s_fold, 1)
            v.tensor_tensor(gg[:, :], F("gsi_p"), F("gsi_q"), ALU.mult).then_inc(s_fold, 1)
            banks = [p_y[0], p_y[1], p_u[0], p_u[1]]
            for t in range(TILES):
                if t % 4 == 0:
                    v.wait_ge(s_xmm, t // 4 + 1)
                v.bn_stats(x_stats[:, t, :], banks[t // 4][:, t % 4 * E:t % 4 * E + E]).then_inc(s_xstat, 1)
            for t in range(TILES):
                v.wait_ge(s_xstat, t + 1)
                v.bn_aggr(x_mv[:, t, :], x_stats[:, t, :]).then_inc(s_xmv, 1)
            v.wait_ge(s_xsd, 1)
            v.reciprocal(x_rs[:, :], x_sd[:, :]).then_inc(s_xrs, 1)
            v.wait_ge(s_xrs, 1)
            for t in range(TILES):
                v.tensor_scalar(xn[:, t, :], banks[t // 4][:, t % 4 * E:t % 4 * E + E], x_mv[:, t, 0:1],
                                x_rs[:, t:t + 1], ALU.subtract, ALU.mult).then_inc(s_xn, 1)
            for b in range(2):
                v.memset(emb_t[b][:, :, :], 0.0).then_inc(s_clear, 1)
            v.wait_ge(s_wsimm, 1)
            v.wait_ge(s_cen, 2)
            v.tensor_copy(wsi_c[:, :], p_o[:, 0:P]).then_inc(s_wsi, 1)
            v.wait_ge(s_foldmm, 1)
            for k in range(ZK):
                added = {SUM_STEP: p_t, ONE_STEP: p_z[0]}.get(k)
                top = P if added is None else WCUT
                last = v.tensor_scalar(wl_sb[0:top, k, :], wl_sb[0:top, k, :], gg[0:top, k:k + 1], None, ALU.mult)
                if added is not None:
                    last = v.scalar_tensor_tensor(wl_sb[WCUT:P, k, :], wl_sb[WCUT:P, k, :], gg[WCUT:P, k:k + 1],
                                                  added[WCUT:P, :], ALU.mult, ALU.add)
                last.then_inc(s_wls, 1)
            v.wait_ge(s_xtr, 4)
            for b in range(2):
                v.memset(feat[b][:, :, ONE_AT:COLS], 1.0)

            def tile(t, known, uses, b=None):
                live = known is None or known < TILES
                prev = known is None or 1 <= known <= TILES
                prev2 = known is None or known >= 2
                b = known % 2 if b is None else b
                o = 1 - b
                for c in range(CHUNKS):
                    s = t * CHUNKS + c
                    q = c % 2
                    if c == 1 and prev2:
                        v.wait_ge(s_l, t - 1)
                        v.bn_stats(l_stats[:, :], p_o[:, :]).then_inc(s_lst, 1)
                        v.wait_ge(s_lst, t - 1)
                    if there(known, c, NORM):
                        need(v, s_squ, s - 1)
                        v.tensor_reduce(ss_u[q][:, :], sq_u[q][:, :].rearrange("p (b q) -> p b q", b=CHUNK),
                                        AX.X, ALU.add).then_inc(s_ssu, 1)
                    if c == 1 and prev2:
                        v.bn_aggr(l_mv[:, :], l_stats[:, :]).then_inc(s_lmv, 1)
                    if live:
                        need(v, s_sqy, s + 1)
                        v.tensor_reduce(ss_y[q][0:ROWS, :],
                                        sq_y[q][0:ROWS, :].rearrange("p (g e) -> p g e", g=4),
                                        AX.X, ALU.add).then_inc(s_ssy, 1)
                    if there(known, c, NORM):
                        fc = (c - NORM) % CHUNKS
                        fb = b if c >= NORM else o
                        need(v, s_sdu, s - 1)
                        v.reciprocal(rs_u[q][:, :], sd_u[q][:, :]).then_inc(s_rsu, 1)
                        if fc == 0:
                            need(v, s_z, (t - 1) * CHUNKS)
                            if known == 0:
                                v.wait_ge(s_xt, 4)
                            v.tensor_copy(feat[fb][:, :, X_AT], x_t[:, bass.ds(t * TILE, TILE)])
                        need(v, s_rsu, s - 1)
                        dst = feat[fb][:, :, 0:PROJ].rearrange("p (g c i) q -> p g c i q", g=4, i=GROUP)
                        v.tensor_tensor(dst[:, :, fc, :, :],
                                        p_u[q][:, :].rearrange("p (g i q) -> p g i q", g=4, i=GROUP),
                                        rs_u[q][:, :].rearrange("p (g i) -> p g i", g=4).unsqueeze(3)
                                        .to_broadcast([P, 4, GROUP, PROJ]), ALU.mult).then_inc(s_feat, 1)
                    if live:
                        need(v, s_sdy, s + 1)
                        v.reciprocal(rs_y[q][0:ROWS, :], sd_y[q][0:ROWS, :]).then_inc(s_rsy, 1)
                        need(v, s_rsy, s + 1)
                        need(v, s_u, s - 1)
                        for g in range(4):
                            last = v.scalar_tensor_tensor(
                                y_sb[q][0:ROWS, g, :], p_y[q][0:ROWS, g * E:g * E + E], rs_y[q][0:ROWS, g:g + 1],
                                F("gs", 0, ROWS), ALU.mult, ALU.mult)
                        last.then_inc(s_ysb, 1)
                    if c == 1 and prev2:
                        v.wait_ge(s_lsd, t - 1)
                        v.reciprocal(l_rs[:, :], l_sd[:, :]).then_inc(s_lrs, 1)
                        v.wait_ge(s_lrs, t - 1)
                        v.tensor_scalar(zn[:, :], p_o[:, 0:USED], l_mv[:, 0:1], l_rs[:, 0:1],
                                        ALU.subtract, ALU.mult).then_inc(s_zn, 1)
                    if c == 5 and prev2:
                        v.wait_ge(s_h2, t - 1)
                        for m in range(H2 // P):
                            last = v.tensor_scalar(h2_t[:, m, :], p_o[:, m * TILE:(m + 1) * TILE],
                                                   F("b2")[:, m:m + 1], 0.0, ALU.add, ALU.max)
                        last.then_inc(s_h2t, 1)
                    if c == 7 and prev2:
                        v.wait_ge(s_o, t - 1)
                        v.tensor_copy(out_sb[0:1, bass.ds((t - 2) * TILE, TILE)], p_t[0:1, 0:TILE]).then_inc(s_osb, 1)

            over_tiles(v, tile)


def kernel(**inputs):
    import concourse.bacc as _bacc
    from concourse.bass_utils import run_bass_kernel_spmd as _run

    a = {name: np.ascontiguousarray(value) for name, value in inputs.items()}
    f32 = np.float32

    tri = {(i, j): i * (i - 1) // 2 + j for i in range(PROJ + 1) for j in range(i)}
    wlT = a["L0_rec_Wl"].T
    wl = np.zeros((P, ZK, MAXD), f32)
    gsi, bsi = a["L0_rec_gsi"], a["L0_rec_bsi"]
    lay = {n: np.zeros((P, ZK), f32) for n in ("bsi_p", "bsi_q", "bsi_x")}
    lay.update({n: np.ones((P, ZK), f32) for n in ("gsi_p", "gsi_q")})
    delta = {n: np.zeros((P, ZK, PROJ), f32) for n in ("delta_p", "delta_q")}

    def pair(row, step, p, q):
        wl[row, step] = wlT[tri[p + 1, q + 1]]
        for kind, at in (("p", p), ("q", q)):
            lay["gsi_" + kind][row, step] = gsi[at]
            lay["bsi_" + kind][row, step] = bsi[at]
            delta["delta_" + kind][row, step, at] = 1.0

    row = 0
    for q0, n in BLOCKS:
        for r in range(n):
            for k in range(min(ZK, r + 1)):
                pair(row + r, k, q0 + 1 + r, q0 + k)
        row += n
    pair(REST_AT + PROJ - 1, 0, PROJ - 1, PROJ - 2)
    for p in range(PROJ):
        r, k = REST_AT + p, X_AT - REST_Q
        wl[r, k] = wlT[tri[p + 1, 0]]
        lay["gsi_p"][r, k] = gsi[p]
        lay["bsi_x"][r, k] = bsi[p]

    prm = np.zeros((P, NPAR), f32)

    def put(name, value, rows=slice(None)):
        lo, hi = FIELD[name]
        prm[rows, lo:hi] = value

    put("ident", np.eye(P, dtype=f32))
    isum = np.zeros((P, P), f32)
    isum[:ROWS, :ROWS] = np.eye(ROWS, dtype=f32)
    isum[:ROWS, ROWS] = 1.0
    put("ident_sum", isum)
    for name, value in lay.items():
        put(name, value)
    for name, value in delta.items():
        put(name, value.reshape(P, ZK * PROJ))
    put("gsi_free", np.tile(gsi, (P, 1)))
    put("ws", np.concatenate([a["L0_rec_Ws"].T, a["L0_rec_Ws"].T]))
    wsi = np.zeros((P, P), f32)
    for g in range(GROUP):
        wsi[NF * g:NF * g + NF, PROJ * g:PROJ * g + PROJ] = a["L0_rec_Wsi"].T
    put("wsi", wsi)
    put("gs", np.tile(a["L0_rec_gs"], (P, 1)))
    put("gd", a["L0_rec_gd"][:, None])
    put("bd", a["L0_rec_bd"][:, None])
    put("gl", a["L0_rec_gl"][:USED].reshape(UK, P).T)
    put("bl", a["L0_rec_bl"][:USED].reshape(UK, P).T)
    put("b1", a["b_top1"].reshape(H1 // P, P).T)
    put("b2", a["b_top2"].reshape(H2 // P, P).T)
    put("w3", a["W_top3"].reshape(H2 // P, P).T)
    put("wd", a["L0_rec_Wd"].T.reshape(DK, P, E).transpose(1, 0, 2).reshape(P, DK * E))

    nc = _bacc.Bacc("TRN2", target_bir_lowering=False, num_devices=1)
    arrays = {f"tbl_{n}_dram": a[f"tbl_{n}"] for n in range(NF)}
    arrays.update(
        ids_dram=a["ids"], params_dram=prm,
        bs_dram=np.tile(a["L0_rec_bs"], (1, 4)).reshape(1, 4, E),
        dense_dram=np.ascontiguousarray(a["r_dense_t"].T), wl_dram=wl,
        w1_dram=a["W_top1"], w2_dram=a["W_top2"])
    ap = {k: nc.dram_tensor(k, x.shape, mybir.dt.from_np(x.dtype), kind="ExternalInput").ap()
          for k, x in arrays.items()}
    out = nc.dram_tensor("out_dram", (BATCH, 1), mybir.dt.float32, kind="ExternalOutput").ap()
    build(nc, [ap[f"tbl_{n}_dram"] for n in range(NF)], ap["ids_dram"], ap["params_dram"], ap["bs_dram"],
          ap["dense_dram"], ap["wl_dram"], ap["w1_dram"], ap["w2_dram"], out)
    r = _run(nc, [arrays], core_ids=[0])
    return r.results[0]["out_dram"]
```

```python
import concourse.bass as bass
import numpy as np
from concourse import mybir
from contextlib import ExitStack

BATCH = 2048
NF = 26
DSP = 64
E = 128
PROJ = 32
DD = 256
MAXD = 512
USED = 384
H1, H2 = 512, 256
EPS = 1e-5

P = 128
TILE = 128
TILES = BATCH // TILE
GROUP = 4
CHUNK = 4 * GROUP
CHUNKS = TILE // CHUNK
ROWS = GROUP * NF
ZK = 6
BLOCKS = [(q, PROJ - 1 - q) for q in range(0, PROJ - ZK + 1, ZK)]
REST_AT = sum(n for _, n in BLOCKS)
REST_Q = ZK * len(BLOCKS)
COLS = REST_Q + ZK
X_AT, ONE_AT = PROJ, PROJ + 1
SUM_STEP, ONE_STEP = ONE_AT - REST_Q, ONE_AT - REST_Q + 1
WCUT = 64
assert REST_AT + PROJ == P - 1 and REST_Q == PROJ - 2 and REST_AT >= WCUT and ONE_STEP < ZK
UK = USED // P
DK = DD // P
PIECES = [(0, 4), (4, 7), (7, 10), (10, 13)]
SLOTS = TILE // 4
MOVES = len(BLOCKS) + 2

_FIELDS = [("ident", P), ("ident_sum", P), ("delta_p", ZK * PROJ), ("delta_q", ZK * PROJ), ("bsi_p", ZK),
           ("bsi_q", ZK), ("bsi_x", ZK), ("gsi_p", ZK), ("gsi_q", ZK), ("gsi_free", PROJ), ("ws", E), ("wsi", P),
           ("gs", E), ("gd", 1), ("bd", 1), ("gl", UK), ("bl", UK), ("b1", H1 // P), ("b2", H2 // P),
           ("w3", H2 // P), ("wd", DK * E)]
FIELD = {}
NPAR = 0
for _name, _width in _FIELDS:
    FIELD[_name] = (NPAR, NPAR + _width)
    NPAR += _width


def build(nc, tables, ids, params, bs_row, dense_t, wl, w1, w2, out):
    fp32 = mybir.dt.float32
    i32 = mybir.dt.int32
    f32r = mybir.dt.float32r
    ALU = mybir.AluOpType
    ACT = mybir.ActivationFunctionType
    AX = mybir.AxisListType

    with ExitStack() as ctx:
        def sb(name, shape, dt=fp32):
            return ctx.enter_context(nc.sbuf_tensor(name, shape, dt))

        def bank(name):
            return ctx.enter_context(nc.psum_tensor(name, [P, 512], fp32))

        def sem(name):
            return ctx.enter_context(nc.semaphore(name))

        par = sb("par", [P, NPAR])
        wl_sb = sb("wl_sb", [P, ZK, MAXD])
        w1_sb = sb("w1_sb", [P, UK + DK, H1])
        w2_sb = sb("w2_sb", [P, H1 // P, H2])
        dense_sb = sb("dense_sb", [P, DK, BATCH])
        wl_hi = sb("wl_hi", [P, ZK, MAXD], f32r)
        wl_lo = sb("wl_lo", [P, ZK, MAXD], f32r)
        fold = sb("fold", [P, 2, ZK, P - WCUT])
        ws_c = sb("ws_c", [P, E])
        wsi_c = sb("wsi_c", [P, P])
        gg = sb("gg", [P, ZK])
        means = sb("means", [P, 8])
        ones = sb("ones", [P, 1])
        eps_sb = sb("eps_sb", [P, 1])
        x_stats = sb("x_stats", [P, TILES, 6])
        x_mv = sb("x_mv", [P, TILES, 2])
        x_sd = sb("x_sd", [P, TILES])
        x_rs = sb("x_rs", [P, TILES])
        x_t = sb("x_t", [P, BATCH])
        x_sum = sb("x_sum", [P, TILES, ZK])
        sum_dram = nc.dram_tensor("sum_dram", (TILES, TILE, ZK), fp32).ap()

        idx_all = sb("idx_all", [P, TILES, NF], i32)

        idx = [sb(f"idx{i}", [P, NF], i32) for i in range(2)]
        emb = [sb(f"emb{i}", [P, NF, DSP]) for i in range(2)]
        emb_t = [sb(f"emb_t{i}", [P, TILE, NF]) for i in range(2)]
        feat = [sb(f"feat{i}", [P, TILE, COLS]) for i in range(2)]
        sq_y = [sb(f"sq_y{i}", [P, 512]) for i in range(2)]
        ss_y = [sb(f"ss_y{i}", [P, 4]) for i in range(2)]
        sd_y = [sb(f"sd_y{i}", [P, 4]) for i in range(2)]
        rs_y = [sb(f"rs_y{i}", [P, 4]) for i in range(2)]
        y_sb = [sb(f"y_sb{i}", [P, 4, E]) for i in range(2)]
        sq_u = [sb(f"sq_u{i}", [P, 512]) for i in range(2)]
        ss_u = [sb(f"ss_u{i}", [P, CHUNK]) for i in range(2)]
        sd_u = [sb(f"sd_u{i}", [P, CHUNK]) for i in range(2)]
        rs_u = [sb(f"rs_u{i}", [P, CHUNK]) for i in range(2)]
        z_stage = [sb(f"z_stage{i}", [P, COLS // ZK, SLOTS, ZK]) for i in range(2)]
        z_k = [sb(f"z_k{i}", [P, 4, SLOTS, ZK]) for i in range(2)]
        z_hi = sb("z_hi", [P, ZK, TILE], f32r)
        z_lo = sb("z_lo", [P, ZK, TILE], f32r)
        z_dram = [nc.dram_tensor(f"z_dram{i}", (4, PROJ, COLS // ZK, SLOTS * ZK), fp32).ap() for i in range(2)]
        zn = sb("zn", [P, USED])
        l_stats = sb("l_stats", [P, 6])
        l_mv = sb("l_mv", [P, 2])
        l_sd = sb("l_sd", [P, 1])
        l_rs = sb("l_rs", [P, 1])
        zn_t = sb("zn_t", [P, UK, TILE])
        h1_t = sb("h1_t", [P, H1 // P, TILE])
        h2_t = sb("h2_t", [P, H2 // P, TILE])
        out_sb = dense_sb[0:1, 0, :]
        pair_sum, pair_q = (zn_t[:, :, :].rearrange("p a b -> p (a b)")[:, i * ZK * PROJ:(i + 1) * ZK * PROJ]
                            .rearrange("p (k r) -> p k r", k=ZK) for i in range(2))
        xn = feat[0][:, :, :].rearrange("p a b -> p (a b)")[:, 0:BATCH].rearrange("p (t e) -> p t e", t=TILES)

        p_y = [bank(f"p_y{i}") for i in range(2)]
        p_u = [bank(f"p_u{i}") for i in range(2)]
        p_z = [bank(f"p_z{i}") for i in range(2)]
        p_t = bank("p_t")
        p_o = bank("p_o")

        def F(name, lo=0, hi=P):
            a, b = FIELD[name]
            return par[lo:hi, a:b]

        s_par = sem("s_par")
        s_dense = sem("s_dense")
        s_wl = sem("s_wl")
        s_w12 = sem("s_w12")
        s_bsrow = sem("s_bsrow")
        s_idxall = [sem(f"s_idxall{i}") for i in range(2)]
        s_gather = [[sem(f"s_gather{i}_{k}") for k in range(len(PIECES))] for i in range(2)]
        s_idx = sem("s_idx")
        s_start = sem("s_start")
        s_clear = sem("s_clear")
        s_xmm = sem("s_xmm")
        s_xstat = sem("s_xstat")
        s_xmv = sem("s_xmv")
        s_xsd = sem("s_xsd")
        s_xrs = sem("s_xrs")
        s_xn = sem("s_xn")
        s_xtr = sem("s_xtr")
        s_xt = sem("s_xt")
        s_xsmm = sem("s_xsmm")
        s_xs = sem("s_xs")
        s_sumd = sem("s_sumd")
        s_mean = sem("s_mean")
        s_cen = sem("s_cen")
        s_wsimm = sem("s_wsimm")
        s_wsi = sem("s_wsi")
        s_fold = sem("s_fold")
        s_foldmm = sem("s_foldmm")
        s_wls = sem("s_wls")
        s_wadd = sem("s_wadd")
        s_whi = sem("s_whi")
        s_wlo = sem("s_wlo")
        s_y = sem("s_y")
        s_ssy = sem("s_ssy")
        s_sdy = sem("s_sdy")
        s_rsy = sem("s_rsy")
        s_ysb = sem("s_ysb")
        s_u = sem("s_u")
        s_squ = sem("s_squ")
        s_ssu = sem("s_ssu")
        s_sdu = sem("s_sdu")
        s_rsu = sem("s_rsu")
        s_feat = sem("s_feat")
        s_z = sem("s_z")
        s_zs = sem("s_zs")
        s_tr = sem("s_tr")
        s_embt = sem("s_embt")
        s_zd = sem("s_zd")
        s_zk = [sem(f"s_zk{i}") for i in range(2)]
        s_zhi = sem("s_zhi")
        s_zlo = sem("s_zlo")
        s_l = sem("s_l")
        s_lst = sem("s_lst")
        s_lmv = sem("s_lmv")
        s_lsd = sem("s_lsd")
        s_lrs = sem("s_lrs")
        s_zn = sem("s_zn")
        s_zt = sem("s_zt")
        s_znt = sem("s_znt")
        s_h1 = sem("s_h1")
        s_h1t = sem("s_h1t")
        s_h2 = sem("s_h2")
        s_h2t = sem("s_h2t")
        s_o = sem("s_o")
        s_osb = sem("s_osb")
        s_out = sem("s_out")

        block = ctx.enter_context(nc.Block())

        def need(eng, s, value):
            if not isinstance(value, int) or value > 0:
                eng.wait_ge(s, value)

        def over_tiles(eng, tile):
            for t in (0, 1):
                tile(t, t, 0)
            with eng.Fori(1, TILES // 2 - 1) as i:
                for par_ in range(2):
                    tile(i * 2 + par_, None, i, par_)
            for t in range(TILES - 2, TILES + 2):
                tile(t, t, t // 2)

        COMBINE, NORM, INTERACT = 1, 2, 4

        def piece_chunk(known):
            return {0: 4, 1: 3}.get(known, 2)

        def rows_of(k):
            return 16 * 2 * (PIECES[k][1] - PIECES[k][0])

        def there(known, c, lag=0):
            return known is None or 0 <= known * CHUNKS + c - lag < TILES * CHUNKS

        @block.sync
        def _(sp):
            by_tile = ids.rearrange("(t p) n -> p t n", p=P)
            sp.dma_start(idx_all[:, 0:1, :], by_tile[:, 0:1, :]).then_inc(s_idxall[0], 16)
            sp.dma_start(par[:, :], params).then_inc(s_par, 16)
            sp.dma_start(idx_all[:, 1:TILES, :], by_tile[:, 1:TILES, :]).then_inc(s_idxall[1], 16)
            sp.dma_start(dense_sb[:, :, :], dense_t.rearrange("(k p) b -> p k b", p=P)).then_inc(s_dense, 16)
            sp.dma_start(wl_sb[:, :, :], wl).then_inc(s_wl, 16)
            for b in range(2):
                sp.dma_start(y_sb[b][ROWS:ROWS + 1, :, :], bs_row).then_inc(s_bsrow, 16)
            sp.dma_start(w1_sb[:, 0:UK, :],
                         w1[0:USED, :].rearrange("(k p) n -> p k n", p=P)).then_inc(s_w12, 16)
            sp.dma_start(w1_sb[:, UK:UK + DK, :],
                         w1[MAXD:MAXD + DD, :].rearrange("(k p) n -> p k n", p=P)).then_inc(s_w12, 16)
            sp.dma_start(w2_sb[:, :, :], w2.rearrange("(k p) n -> p k n", p=P)).then_inc(s_w12, 16)
            sp.wait_ge(s_xs, 1)
            sp.dma_start(sum_dram.rearrange("t b k -> b t k"), x_sum[:, :, :]).then_inc(s_sumd, 16)
            sp.wait_ge(s_sumd, 16)
            sums = sum_dram.rearrange("t b k -> t (b k)")

            def held(value):
                return value if isinstance(value, int) else sp.snap(value)

            def tile(t, known, uses, b=None):
                b = known % 2 if b is None else b
                if known is None or 1 <= known <= TILES:
                    o = 1 - b
                    staged, row = held(t * CHUNKS), held(t - 1)
                    need(sp, s_zs, staged)
                    sp.dma_start(z_dram[o].rearrange("g p j n -> (g p) (j n)"),
                                 z_stage[o][:, :, :, :].rearrange("p j i q -> p (j i q)")).then_inc(s_zd, 16)
                    sp.wait_ge(s_zd, t * 16)
                    src = z_dram[o].rearrange("g p j n -> p j g n")
                    dst = z_k[o][:, :, :, :].rearrange("p g i q -> p g (i q)")
                    at = 0
                    for j, (q, n) in enumerate(BLOCKS):
                        sp.dma_start(dst[at:at + n, :, :], src[q + 1:q + 1 + n, j, :, :]).then_inc(s_zk[o], 16)
                        at += n
                    sp.dma_start(dst[at:at + PROJ, :, :], src[:, len(BLOCKS), :, :]).then_inc(s_zk[o], 16)
                    sp.dma_start(dst[P - 1:P, :, :].rearrange("p g n -> p (g n)"),
                                 sums[bass.ds(row, 1), :]).then_inc(s_zk[o], 16)

            over_tiles(sp, tile)
            sp.wait_ge(s_osb, TILES)
            sp.dma_start(out.rearrange("b a -> a b"), out_sb).then_inc(s_out, 16)
            sp.wait_ge(s_out, 16)

        @block.gpsimd
        def _(pool):
            def tile(t, known, uses, b=None):
                if known is not None and known >= TILES:
                    return
                b = known % 2 if b is None else b
                if known is not None and known < 2:
                    pool.wait_ge(s_idxall[known], 16)
                need(pool, s_tr, (t - 1) * len(PIECES))
                pool.tensor_copy(idx[b][:, :], idx_all[:, t, :]).then_inc(s_idx, 1)
                pool.wait_ge(s_idx, t + 1)
                pool.sem_inc(s_start, 1)
                for k, (a, z) in enumerate(PIECES):
                    for n in range(2 * a, 2 * z):
                        pool.indirect_dma_start(
                            emb[b][:, n, :], None, tables[n],
                            bass.IndirectOffsetOnAxis(ap=idx[b][:, n:n + 1], axis=0)).then_inc(s_gather[b][k], 16)

            over_tiles(pool, tile)

        @block.tensor
        def _(pe):
            banks = [p_y[0], p_y[1], p_u[0], p_u[1]]
            pe.wait_ge(s_par, 16)
            pe.wait_ge(s_dense, 16)
            wd = F("wd").rearrange("p (k e) -> p k e", k=DK)
            for q in range(4):
                for i in range(4):
                    t = 4 * q + i
                    for k in range(DK):
                        last = pe.matmul(banks[q][:, i * E:i * E + E], dense_sb[:, k, t * TILE:t * TILE + TILE],
                                         wd[:, k, :], start=(k == 0), stop=(k == DK - 1))
                last.then_inc(s_xmm, 1)
            pe.wait_ge(s_cen, 2)
            pe.matmul(p_o[:, 0:P], F("ident_sum", 0, ROWS), wsi_c[0:ROWS, :], start=True, stop=True).then_inc(s_wsimm, 1)

            def transposes(t, b, k, uses):
                pe.wait_ge(s_gather[b][k], (uses + 1) * rows_of(k))
                need(pe, s_embt, (t * len(PIECES) + k) * 2)
                if k == 0:
                    need(pe, s_osb, t - 3)
                a, z = PIECES[k]
                for n in range(a, z):
                    last = pe.transpose(p_t[:, (n - a) * TILE:(n - a + 1) * TILE],
                                        emb[b][:, 2 * n:2 * n + 2, :].rearrange("p n d -> p (n d)"), F("ident"))
                last.then_inc(s_tr, 1)

            for k in (0, 1):
                transposes(0, 0, k, 0)
            pe.wait_ge(s_wl, 16)
            pe.wait_ge(s_fold, 7)
            for m, dst in enumerate(p_z):
                for k in range(ZK):
                    last = pe.matmul(dst[WCUT:P, :], fold[:, m, k, :], wl_sb[:, k, :],
                                     start=(k == 0), stop=(k == ZK - 1))
            last.then_inc(s_foldmm, 1)
            for k in (2, 3):
                for q in (2 * (k - 2), 2 * (k - 2) + 1):
                    pe.wait_ge(s_xn, 4 * (q + 1))
                    for i in range(4):
                        last = pe.transpose(banks[q][:, i * TILE:i * TILE + TILE], xn[:, 4 * q + i, :], F("ident"))
                    last.then_inc(s_xtr, 1)
                transposes(0, 0, k, 0)
            pe.wait_ge(s_bsrow, 32)

            def project(s, c, b):
                for g in range(4):
                    e0 = g * SLOTS + c * GROUP
                    last = pe.matmul(p_y[c % 2][0:ROWS, g * E:g * E + E],
                                     emb_t[b][:, e0:e0 + GROUP, :].rearrange("p a b -> p (a b)"),
                                     ws_c[:, :], start=True, stop=True)
                last.then_inc(s_y, 1)

            def combine(c):
                for g in range(4):
                    last = pe.matmul(p_u[c % 2][:, g * P:g * P + P], y_sb[c % 2][0:ROWS + 1, g, :],
                                     wsi_c[0:ROWS + 1, :], start=True, stop=True)
                last.then_inc(s_u, 1)

            def interact(c, b):
                for e in range(CHUNK):
                    i, g = e // 4, e % 4
                    v = feat[b][:, g * SLOTS + c * GROUP + i, :]
                    last = pe.matmul(p_z[c % 2][32 * g:32 * g + 32, i * COLS:(i + 1) * COLS],
                                     v[:, 0:PROJ], v, start=True, stop=True)
                last.then_inc(s_z, 1)

            def layer(lhs, rhs, first=False, final=False):
                for k in range(ZK):
                    last = pe.matmul(p_o[:, :], lhs[:, k, :], rhs[:, k, :],
                                     start=first and k == 0, stop=final and k == ZK - 1)
                if final:
                    last.then_inc(s_l, 1)

            def tile(t, known, uses, b=None):
                live = known is None or known < TILES
                nxt = known is None or known + 1 < TILES
                prev = known is None or 1 <= known <= TILES
                prev2 = known is None or known >= 2
                b = known % 2 if b is None else b
                o = 1 - b
                for c in range(CHUNKS):
                    s = t * CHUNKS + c
                    if live:
                        if c == 0:
                            need(pe, s_embt, (t + 1) * (2 * len(PIECES)))
                        need(pe, s_ysb, s - 1)
                        project(s, c, b)
                    if there(known, c, INTERACT):
                        if known == 0 and c == INTERACT:
                            pe.wait_ge(s_wadd, 2)
                        need(pe, s_feat, s - 3)
                        need(pe, s_zs, s - 5)
                        if c == 4 and prev2:
                            pe.wait_ge(s_znt, (t - 1) * UK)
                        interact((c - INTERACT) % CHUNKS, b if c >= INTERACT else o)
                    if c < 4 and known == 0:
                        pe.wait_ge(s_clear, 1)
                        pe.wait_ge(s_wsi, 1)
                        pe.wait_ge(s_xt, c + 1)
                        for n in range(4 * c, 4 * c + 4):
                            last = pe.matmul(p_o[:, n:n + 1], x_t[:, n * TILE:(n + 1) * TILE], ones[:, :],
                                             start=True, stop=True)
                        last.then_inc(s_xsmm, 1)
                    if c == 0 and prev2:
                        layer(z_hi, wl_lo)
                    if c == 1 and prev2:
                        pe.wait_ge(s_zlo, t - 1)
                        layer(z_lo, wl_hi, final=True)
                    if c == 3 and prev2:
                        pe.wait_ge(s_zn, t - 1)
                        pe.wait_ge(s_zs, s - 4 if known is None else min(s - 4, TILES * CHUNKS))
                        for k in range(UK):
                            last = pe.transpose(p_z[0][:, k * TILE:(k + 1) * TILE], zn[:, k * P:(k + 1) * P], F("ident"))
                        last.then_inc(s_zt, 1)
                    if c in (4, 5) and prev2:
                        if c == 4:
                            pe.wait_ge(s_w12, 48)
                            pe.wait_ge(s_znt, (t - 1) * UK)
                        for m in range(2 * (c - 4), 2 * (c - 3)):
                            for k in range(UK + DK):
                                rhs = zn_t[:, k, :] if k < UK else dense_sb[:, k - UK, bass.ds((t - 2) * TILE, TILE)]
                                last = pe.matmul(p_o[:, m * TILE:(m + 1) * TILE], w1_sb[:, k, m * P:(m + 1) * P],
                                                 rhs, start=(k == 0), stop=(k == UK + DK - 1))
                        if c == 5:
                            last.then_inc(s_h1, 1)
                    if c == 6 and prev2:
                        pe.wait_ge(s_h1t, (t - 1) * (H1 // P))
                        for m in range(H2 // P):
                            for k in range(H1 // P):
                                last = pe.matmul(p_o[:, m * TILE:(m + 1) * TILE], w2_sb[:, k, m * P:(m + 1) * P],
                                                 h1_t[:, k, :], start=(k == 0), stop=(k == H1 // P - 1))
                        last.then_inc(s_h2, 1)
                    if c == 7 and prev:
                        pe.wait_ge(s_zhi, t)
                        pe.wait_ge(s_wlo, ZK)
                        need(pe, s_h2t, t - 1)
                        layer(z_hi, wl_hi, first=True)
                    k = c - piece_chunk(known)
                    if 0 <= k < len(PIECES) and nxt:
                        nuses = (known + 1) // 2 if known is not None else uses + b
                        transposes(t + 1, o, k, nuses)
                    if c == 7 and prev2:
                        pe.wait_ge(s_h2t, t - 1)
                        pe.wait_ge(s_embt, min(t + 2, TILES) * 2 * len(PIECES) if known is not None
                                   else (t + 2) * (2 * len(PIECES)))
                        for k in range(H2 // P):
                            last = pe.matmul(p_t[0:1, 0:TILE], F("w3")[:, k:k + 1], h2_t[:, k, :],
                                             start=(k == 0), stop=(k == H2 // P - 1))
                        last.then_inc(s_o, 1)
                    if there(known, c, COMBINE):
                        need(pe, s_ysb, s)
                        need(pe, s_feat, s - 2)
                        combine((c - COMBINE) % CHUNKS)

            over_tiles(pe, tile)

        @block.scalar
        def _(act):
            act.wait_ge(s_clear, 1)
            act.activation(x_sd[:, 0:1], eps_sb[:, 0:1], ACT.Sqrt)

            def land(t, k, b):
                need(act, s_tr, t * len(PIECES) + k + 1)
                a, z = PIECES[k]
                src = p_t[:, 0:(z - a) * TILE].rearrange("p (n b) -> p n b", n=z - a)
                for h in range(2):
                    dst = emb_t[b][64 * h:64 * h + 64, :, 2 * a + h:2 * z:2].rearrange("p b n -> p n b")
                    act.activation(dst, src[64 * h:64 * h + 64, :, :], ACT.Copy).then_inc(s_embt, 1)

            act.wait_ge(s_clear, 3)
            for k in (0, 1):
                land(0, k, 0)
            act.wait_ge(s_xmv, TILES)
            act.activation(x_sd[:, :], x_mv[:, :, 1], ACT.Sqrt, bias=eps_sb[:, 0:1]).then_inc(s_xsd, 1)
            banks = [p_y[0], p_y[1], p_u[0], p_u[1]]
            for k in (2, 3):
                for q in (2 * (k - 2), 2 * (k - 2) + 1):
                    act.wait_ge(s_xtr, q + 1)
                    act.activation(x_t[:, 512 * q:512 * q + 512], banks[q][:, :], ACT.Identity,
                                   scale=F("gd"), bias=F("bd")).then_inc(s_xt, 1)
                land(0, k, 0)

            def tile(t, known, uses, b=None):
                live = known is None or known < TILES
                nxt = known is None or known + 1 < TILES
                prev = known is None or 1 <= known <= TILES
                prev2 = known is None or known >= 2
                b = known % 2 if b is None else b
                o = 1 - b
                for c in range(CHUNKS):
                    s = t * CHUNKS + c
                    q = c % 2
                    if there(known, c, NORM):
                        need(act, s_u, s - 1)
                        need(act, s_ssu, s - 3)
                        act.activation(sq_u[q][:, :], p_u[q][:, :], ACT.Square).then_inc(s_squ, 1)
                    if live:
                        need(act, s_y, s + 1)
                        need(act, s_rsy, s - 1)
                        for g in range(4):
                            last = act.activation(sq_y[q][0:ROWS, g * E:g * E + E], p_y[q][0:ROWS, g * E:g * E + E],
                                                  ACT.Square, accum_out=ss_y[q][0:ROWS, g:g + 1])
                        last.then_inc(s_ssy, 1)
                    if live:
                        need(act, s_ssy, s + 1)
                        act.activation(sd_y[q][0:ROWS, :], ss_y[q][0:ROWS, :], ACT.Sqrt, scale=1.0 / E,
                                       bias=eps_sb[0:ROWS, 0:1]).then_inc(s_sdy, 1)
                    if c == 3 and prev2:
                        act.wait_ge(s_zt, t - 1)
                        need(act, s_h1, t - 2)
                        for k in range(UK):
                            act.activation(zn_t[:, k, :], p_z[0][:, k * TILE:(k + 1) * TILE], ACT.Identity,
                                           scale=F("gl")[:, k:k + 1], bias=F("bl")[:, k:k + 1]).then_inc(s_znt, 1)
                    if there(known, c, NORM):
                        need(act, s_ssu, s - 1)
                        need(act, s_rsu, s - 3)
                        act.activation(sd_u[q][:, :], ss_u[q][:, :], ACT.Sqrt, scale=1.0 / PROJ,
                                       bias=eps_sb[:, 0:1]).then_inc(s_sdu, 1)
                    if there(known, c, INTERACT):
                        zb = b if c >= INTERACT else o
                        zc = (c - INTERACT) % CHUNKS
                        need(act, s_z, s - 3)
                        if zc == 0:
                            need(act, s_zk[zb], uses * (16 * MOVES))
                        act.activation(
                            z_stage[zb][:, :, zc * GROUP:(zc + 1) * GROUP, :].rearrange("p j i q -> p i j q"),
                            p_z[q][:, 0:GROUP * COLS].rearrange("p (i j q) -> p i j q", i=GROUP, q=ZK),
                            ACT.Copy).then_inc(s_zs, 1)
                    if c == 3 and known == 0:
                        act.wait_ge(s_xsmm, 4)
                        act.activation(x_sum[:, :, SUM_STEP], p_o[:, 0:TILES], ACT.Copy).then_inc(s_xs, 1)
                    if known == 0 and 1 <= c <= ZK:
                        act.wait_ge(s_wls, c)
                        act.wait_ge(s_wadd, 2)
                        act.activation(wl_hi[:, c - 1, :], wl_sb[:, c - 1, :], ACT.Copy).then_inc(s_whi, 1)
                    if c == 1 and prev2:
                        act.wait_ge(s_lmv, t - 1)
                        act.activation(l_sd[:, :], l_mv[:, 1:2], ACT.Sqrt, bias=eps_sb[:, 0:1]).then_inc(s_lsd, 1)
                    if c == 5 and prev2:
                        act.wait_ge(s_h1, t - 1)
                        need(act, s_h2, t - 2)
                        for m in range(H1 // P):
                            act.activation(h1_t[:, m, :], p_o[:, m * TILE:(m + 1) * TILE], ACT.Relu,
                                           bias=F("b1")[:, m:m + 1]).then_inc(s_h1t, 1)
                    if c == 5 and prev:
                        spread = (known + 1) // 2 if known is not None else uses + b
                        act.wait_ge(s_zk[o], spread * (16 * MOVES))
                        need(act, s_l, t - 1)
                        act.activation(z_hi[:, :, :].rearrange("p k n -> p n k"),
                                       z_k[o][:, :, :, :].rearrange("p g i k -> p (g i) k"), ACT.Copy).then_inc(s_zhi, 1)
                    k = c - piece_chunk(known)
                    if 0 <= k < len(PIECES) and nxt:
                        land(t + 1, k, o)

            over_tiles(act, tile)

        @block.vector
        def _(v):
            v.memset(ones[:, :], 1.0)
            v.memset(x_sum[:, :, :], 1.0)
            v.memset(eps_sb[:, :], EPS).then_inc(s_clear, 1)
            v.memset(emb_t[0][:, :, :], 0.0).then_inc(s_clear, 1)
            v.wait_ge(s_par, 16)
            v.tensor_reduce(means[:, 0:1], F("ws"), AX.X, ALU.add).then_inc(s_mean, 1)
            wsi3 = F("wsi").rearrange("p (g q) -> p g q", g=GROUP)
            v.tensor_reduce(means[:, 2:6], wsi3, AX.X, ALU.add).then_inc(s_mean, 1)
            v.wait_ge(s_mean, 2)
            v.tensor_scalar(means[:, 0:1], means[:, 0:1], 1.0 / E, None, ALU.mult).then_inc(s_mean, 1)
            v.tensor_scalar(means[:, 2:6], means[:, 2:6], 1.0 / PROJ, None, ALU.mult).then_inc(s_mean, 1)
            v.wait_ge(s_mean, 4)
            v.tensor_scalar(ws_c[:, :], F("ws"), means[:, 0:1], None, ALU.subtract).then_inc(s_cen, 1)
            v.tensor_tensor(wsi_c[:, :].rearrange("p (g q) -> p g q", g=GROUP), wsi3,
                            means[:, 2:6].unsqueeze(2).to_broadcast([P, GROUP, PROJ]), ALU.subtract).then_inc(s_cen, 1)
            v.memset(fold[:, :, :, :], 0.0).then_inc(s_fold, 1)
            v.wait_ge(s_fold, 1)
            lo = REST_AT - WCUT
            S = pair_sum
            v.tensor_tensor(S, F("delta_p").rearrange("p (k r) -> p k r", k=ZK),
                            F("bsi_q").unsqueeze(2).to_broadcast([P, ZK, PROJ]), ALU.mult).then_inc(s_fold, 1)
            v.tensor_tensor(pair_q, F("delta_q").rearrange("p (k r) -> p k r", k=ZK),
                            F("bsi_p").unsqueeze(2).to_broadcast([P, ZK, PROJ]), ALU.mult).then_inc(s_fold, 1)
            v.wait_ge(s_fold, 3)
            v.tensor_tensor(S, S, pair_q, ALU.add).then_inc(s_fold, 1)
            v.wait_ge(s_fold, 4)
            v.tensor_tensor(fold[:, 0, :, lo:lo + PROJ], S, F("gsi_free").unsqueeze(1).to_broadcast([P, ZK, PROJ]),
                            ALU.mult)
            v.tensor_copy(fold[:, 0, :, P - WCUT - 1], F("bsi_x")).then_inc(s_fold, 1)
            v.scalar_tensor_tensor(fold[:, 1, :, P - WCUT - 1], F("bsi_p"), float(E), F("bsi_q"),
                                   ALU.mult, ALU.mult).then_inc(s_fold, 1)
            v.tensor_tensor(gg[:, :], F("gsi_p"), F("gsi_q"), ALU.mult).then_inc(s_fold, 1)
            v.memset(emb_t[1][:, :, :], 0.0).then_inc(s_clear, 1)
            banks = [p_y[0], p_y[1], p_u[0], p_u[1]]
            for t in range(TILES):
                if t % 4 == 0:
                    v.wait_ge(s_xmm, t // 4 + 1)
                v.bn_stats(x_stats[:, t, :], banks[t // 4][:, t % 4 * E:t % 4 * E + E]).then_inc(s_xstat, 1)
            for t in range(TILES):
                v.wait_ge(s_xstat, t + 1)
                v.bn_aggr(x_mv[:, t, :], x_stats[:, t, :]).then_inc(s_xmv, 1)
            v.wait_ge(s_wsimm, 1)
            v.wait_ge(s_cen, 2)
            v.tensor_copy(wsi_c[:, :], p_o[:, 0:P]).then_inc(s_wsi, 1)
            v.wait_ge(s_xsd, 1)
            v.reciprocal(x_rs[:, :], x_sd[:, :]).then_inc(s_xrs, 1)
            v.wait_ge(s_xrs, 1)
            for t in range(TILES):
                v.tensor_scalar(xn[:, t, :], banks[t // 4][:, t % 4 * E:t % 4 * E + E], x_mv[:, t, 0:1],
                                x_rs[:, t:t + 1], ALU.subtract, ALU.mult).then_inc(s_xn, 1)
            v.wait_ge(s_foldmm, 1)
            for k, added in ((SUM_STEP, p_z[0]), (ONE_STEP, p_z[1])):
                v.scalar_tensor_tensor(wl_sb[WCUT:P, k, :], wl_sb[WCUT:P, k, :], gg[WCUT:P, k:k + 1],
                                       added[WCUT:P, :], ALU.mult, ALU.add).then_inc(s_wadd, 1)
            v.wait_ge(s_xtr, 4)
            for b in range(2):
                v.memset(feat[b][:, :, ONE_AT:COLS], 1.0)

            def tile(t, known, uses, b=None):
                live = known is None or known < TILES
                prev = known is None or 1 <= known <= TILES
                prev2 = known is None or known >= 2
                b = known % 2 if b is None else b
                o = 1 - b
                for c in range(CHUNKS):
                    s = t * CHUNKS + c
                    q = c % 2
                    if there(known, c, NORM):
                        need(v, s_squ, s - 1)
                        v.tensor_reduce(ss_u[q][:, :], sq_u[q][:, :].rearrange("p (b q) -> p b q", b=CHUNK),
                                        AX.X, ALU.add).then_inc(s_ssu, 1)
                    if live:
                        need(v, s_sdy, s + 1)
                        v.reciprocal(rs_y[q][0:ROWS, :], sd_y[q][0:ROWS, :]).then_inc(s_rsy, 1)
                        need(v, s_rsy, s + 1)
                        need(v, s_u, s - 1)
                        for g in range(4):
                            last = v.scalar_tensor_tensor(
                                y_sb[q][0:ROWS, g, :], p_y[q][0:ROWS, g * E:g * E + E], rs_y[q][0:ROWS, g:g + 1],
                                F("gs", 0, ROWS), ALU.mult, ALU.mult)
                        last.then_inc(s_ysb, 1)
                    if c == 6 and prev2:
                        v.wait_ge(s_h2, t - 1)
                        for m in range(H2 // P):
                            last = v.tensor_scalar(h2_t[:, m, :], p_o[:, m * TILE:(m + 1) * TILE],
                                                   F("b2")[:, m:m + 1], 0.0, ALU.add, ALU.max)
                        last.then_inc(s_h2t, 1)
                    if c == 1 and prev2:
                        v.wait_ge(s_l, t - 1)
                        v.bn_stats(l_stats[:, :], p_o[:, :]).then_inc(s_lst, 1)
                        v.wait_ge(s_lst, t - 1)
                    if there(known, c, NORM):
                        fc = (c - NORM) % CHUNKS
                        fb = b if c >= NORM else o
                        need(v, s_sdu, s - 1)
                        v.reciprocal(rs_u[q][:, :], sd_u[q][:, :]).then_inc(s_rsu, 1)
                    if c == 1 and prev2:
                        v.bn_aggr(l_mv[:, :], l_stats[:, :]).then_inc(s_lmv, 1)
                    if there(known, c, NORM):
                        if fc == 0:
                            need(v, s_z, (t - 1) * CHUNKS)
                            if known == 0:
                                v.wait_ge(s_xt, 4)
                            v.tensor_copy(feat[fb][:, :, X_AT], x_t[:, bass.ds(t * TILE, TILE)])
                        need(v, s_rsu, s - 1)
                        dst = feat[fb][:, :, 0:PROJ].rearrange("p (g c i) q -> p g c i q", g=4, i=GROUP)
                        v.tensor_tensor(dst[:, :, fc, :, :],
                                        p_u[q][:, :].rearrange("p (g i q) -> p g i q", g=4, i=GROUP),
                                        rs_u[q][:, :].rearrange("p (g i) -> p g i", g=4).unsqueeze(3)
                                        .to_broadcast([P, 4, GROUP, PROJ]), ALU.mult).then_inc(s_feat, 1)
                    if known == 0 and c < ZK:
                        top = WCUT if c in (SUM_STEP, ONE_STEP) else P
                        v.tensor_scalar(wl_sb[0:top, c, :], wl_sb[0:top, c, :], gg[0:top, c:c + 1], None,
                                        ALU.mult).then_inc(s_wls, 1)
                    if known == 0 and 2 <= c <= ZK + 1:
                        v.wait_ge(s_whi, c - 1)
                        v.tensor_tensor(wl_lo[:, c - 2, :], wl_sb[:, c - 2, :], wl_hi[:, c - 2, :].bitcast(fp32),
                                        ALU.subtract).then_inc(s_wlo, 1)
                    if c == 1 and prev2:
                        v.wait_ge(s_lsd, t - 1)
                        v.reciprocal(l_rs[:, :], l_sd[:, :]).then_inc(s_lrs, 1)
                        v.wait_ge(s_lrs, t - 1)
                        v.tensor_scalar(zn[:, :], p_o[:, 0:USED], l_mv[:, 0:1], l_rs[:, 0:1],
                                        ALU.subtract, ALU.mult).then_inc(s_zn, 1)
                    if c == 6 and prev:
                        v.wait_ge(s_zhi, t)
                        v.tensor_tensor(z_lo[:, :, :].rearrange("p k n -> p n k"),
                                        z_k[o][:, :, :, :].rearrange("p g i k -> p (g i) k"),
                                        z_hi[:, :, :].bitcast(fp32).rearrange("p k n -> p n k"),
                                        ALU.subtract).then_inc(s_zlo, 1)
                    if c == 7 and prev2:
                        v.wait_ge(s_o, t - 1)
                        v.tensor_copy(dense_sb[0:1, 0, bass.ds((t - 2) * TILE, TILE)], p_t[0:1, 0:TILE]).then_inc(s_osb, 1)

            over_tiles(v, tile)


def kernel(**inputs):
    import concourse.bacc as _bacc
    from concourse.bass_utils import run_bass_kernel_spmd as _run

    a = {name: np.ascontiguousarray(value) for name, value in inputs.items()}
    f32 = np.float32

    tri = {(i, j): i * (i - 1) // 2 + j for i in range(PROJ + 1) for j in range(i)}
    wlT = a["L0_rec_Wl"].T
    wl = np.zeros((P, ZK, MAXD), f32)
    gsi, bsi = a["L0_rec_gsi"], a["L0_rec_bsi"]
    lay = {n: np.zeros((P, ZK), f32) for n in ("bsi_p", "bsi_q", "bsi_x")}
    lay.update({n: np.ones((P, ZK), f32) for n in ("gsi_p", "gsi_q")})
    delta = {n: np.zeros((P, ZK, PROJ), f32) for n in ("delta_p", "delta_q")}

    def pair(row, step, p, q):
        wl[row, step] = wlT[tri[p + 1, q + 1]]
        for kind, at in (("p", p), ("q", q)):
            lay["gsi_" + kind][row, step] = gsi[at]
            lay["bsi_" + kind][row, step] = bsi[at]
            delta["delta_" + kind][row, step, at] = 1.0

    row = 0
    for q0, n in BLOCKS:
        for r in range(n):
            for k in range(min(ZK, r + 1)):
                pair(row + r, k, q0 + 1 + r, q0 + k)
        row += n
    pair(REST_AT + PROJ - 1, 0, PROJ - 1, PROJ - 2)
    for p in range(PROJ):
        r, k = REST_AT + p, X_AT - REST_Q
        wl[r, k] = wlT[tri[p + 1, 0]]
        lay["gsi_p"][r, k] = gsi[p]
        lay["bsi_x"][r, k] = bsi[p]

    prm = np.zeros((P, NPAR), f32)

    def put(name, value, rows=slice(None)):
        lo, hi = FIELD[name]
        prm[rows, lo:hi] = value

    put("ident", np.eye(P, dtype=f32))
    isum = np.zeros((P, P), f32)
    isum[:ROWS, :ROWS] = np.eye(ROWS, dtype=f32)
    isum[:ROWS, ROWS] = 1.0
    put("ident_sum", isum)
    for name, value in lay.items():
        put(name, value)
    for name, value in delta.items():
        put(name, value.reshape(P, ZK * PROJ))
    put("gsi_free", np.tile(gsi, (P, 1)))
    put("ws", np.concatenate([a["L0_rec_Ws"].T, a["L0_rec_Ws"].T]))
    wsi = np.zeros((P, P), f32)
    for g in range(GROUP):
        wsi[NF * g:NF * g + NF, PROJ * g:PROJ * g + PROJ] = a["L0_rec_Wsi"].T
    put("wsi", wsi)
    put("gs", np.tile(a["L0_rec_gs"], (P, 1)))
    put("gd", a["L0_rec_gd"][:, None])
    put("bd", a["L0_rec_bd"][:, None])
    put("gl", a["L0_rec_gl"][:USED].reshape(UK, P).T)
    put("bl", a["L0_rec_bl"][:USED].reshape(UK, P).T)
    put("b1", a["b_top1"].reshape(H1 // P, P).T)
    put("b2", a["b_top2"].reshape(H2 // P, P).T)
    put("w3", a["W_top3"].reshape(H2 // P, P).T)
    put("wd", a["L0_rec_Wd"].T.reshape(DK, P, E).transpose(1, 0, 2).reshape(P, DK * E))

    nc = _bacc.Bacc("TRN2", target_bir_lowering=False, num_devices=1)
    arrays = {f"tbl_{n}_dram": a[f"tbl_{n}"] for n in range(NF)}
    arrays.update(
        ids_dram=a["ids"], params_dram=prm,
        bs_dram=np.tile(a["L0_rec_bs"], (1, 4)).reshape(1, 4, E),
        dense_dram=np.ascontiguousarray(a["r_dense_t"].T), wl_dram=wl,
        w1_dram=a["W_top1"], w2_dram=a["W_top2"])
    ap = {k: nc.dram_tensor(k, x.shape, mybir.dt.from_np(x.dtype), kind="ExternalInput").ap()
          for k, x in arrays.items()}
    out = nc.dram_tensor("out_dram", (BATCH, 1), mybir.dt.float32, kind="ExternalOutput").ap()
    build(nc, [ap[f"tbl_{n}_dram"] for n in range(NF)], ap["ids_dram"], ap["params_dram"], ap["bs_dram"],
          ap["dense_dram"], ap["wl_dram"], ap["w1_dram"], ap["w2_dram"], out)
    r = _run(nc, [arrays], core_ids=[0])
    return r.results[0]["out_dram"]
```
